# Optimizing a Trainium2 kernel written in Bass

```python
import numpy as np
import jax
import jax.numpy as jnp

def _softmax(x, axis=-1):
    return jax.nn.softmax(x, axis=axis)

def _gelu(x):
    return jax.nn.gelu(x, approximate=True)

def _silu(x):
    return jax.nn.silu(x)

def _sigmoid(x):
    return jax.nn.sigmoid(x)

def _layernorm(x, axis=-1, eps=1e-05):
    m = jnp.mean(x, axis=axis, keepdims=True)
    v = jnp.var(x, axis=axis, keepdims=True)
    return (x - m) / jnp.sqrt(v + eps)

def _scatter_add(tgt, idx, src, axis=0):
    return tgt.at[idx].add(src)

def _segment_sum(src, seg, n):
    return jax.ops.segment_sum(src, seg, n)
kernel_name = 'mk_macaron_d1_jaxref_r8_c07d61'

def setup_inputs(seed: int=0):
    np.random.seed(seed)
    _w = jnp.asarray

    def _L0_attn_setup():
        import jax, jax.numpy as jnp
        import numpy as np
        D_MODEL, D_INNER, D_STATE, DT_RANK, D_CONV = (128, 256, 16, 64, 4)
        B, L = (2, 256)

        def _rmsnorm(x, w, eps=1e-05):
            return x * jax.lax.rsqrt(jnp.mean(x * x, axis=-1, keepdims=True) + eps) * w

        def _causal_depthwise_conv(x, conv_w, conv_b):
            K = conv_w.shape[1]
            xp = jnp.pad(x, ((0, 0), (K - 1, 0), (0, 0)))
            Lx = x.shape[1]
            out = conv_b
            for k in range(K):
                out = out + xp[:, k:k + Lx, :] * conv_w[:, k]
            return out

        def _selective_scan(x, delta, Bm, Cm, A):
            h0 = jnp.zeros((x.shape[0], A.shape[0], A.shape[1]), x.dtype)

            def step(h, inp):
                xt, dt, bt, ct = inp
                A_bar = jnp.exp(dt[..., None] * A)
                h = A_bar * h + (dt * xt)[..., None] * bt[:, None, :]
                y = jnp.einsum('ben,bn->be', h, ct)
                return (h, y)
            xs = tuple((jnp.swapaxes(a, 0, 1) for a in (x, delta, Bm, Cm)))
            _, ys = jax.lax.scan(step, h0, xs)
            return jnp.swapaxes(ys, 0, 1)
        key = jax.random.key(seed)
        ks = jax.random.split(key, 14)
        s = lambda k, shp, fan: jax.random.normal(k, shp, jnp.float32) / np.sqrt(fan)
        return {'resid': jax.random.normal(ks[0], (B, L, D_MODEL), jnp.float32), 'norm_w': jnp.ones((D_MODEL,), jnp.float32), 'skip_w': s(ks[1], (D_INNER, D_MODEL), D_MODEL), 'in_w': s(ks[2], (D_INNER, D_MODEL), D_MODEL), 'conv_w': s(ks[3], (D_INNER, D_CONV), D_CONV), 'conv_b': jnp.zeros((D_INNER,), jnp.float32), 'wd1': s(ks[4], (DT_RANK, D_INNER), D_INNER), 'wd2': s(ks[5], (D_INNER, DT_RANK), DT_RANK), 'wd2_b': jnp.zeros((D_INNER,), jnp.float32), 'wb': s(ks[6], (D_STATE, D_INNER), D_INNER), 'wc': s(ks[7], (D_STATE, D_INNER), D_INNER), 'A_log': jax.random.normal(ks[8], (D_INNER, D_STATE), jnp.float32), 'W_D': jnp.ones((D_INNER,), jnp.float32), 'out_w': s(ks[9], (D_MODEL, D_INNER), D_INNER)}
    _L0_attn_in = _L0_attn_setup()

    def _L0_ffn_setup():
        import jax, jax.numpy as jnp
        import numpy as np
        B, S, D, F, E = (1, 128, 128, 512, 8)
        EPS = 1e-05

        def _sublayer(xs, g, b, W1e, b1e, W2e, b2e):
            mu = jnp.mean(xs, axis=-1, keepdims=True)
            var = jnp.mean(jnp.square(xs - mu), axis=-1, keepdims=True)
            h = (xs - mu) * jax.lax.rsqrt(var + EPS) * g + b
            return xs + jax.nn.relu(h @ W1e.T + b1e) @ W2e.T + b2e
        key = jax.random.key(seed)
        ks = jax.random.split(key, 4)
        x = jax.random.normal(ks[0], (B, S, D), jnp.float32)
        centroids = jax.random.normal(ks[1], (E, D), jnp.float32) * 0.1
        gamma = jnp.ones((E, D), jnp.float32)
        beta = jnp.zeros((E, D), jnp.float32)
        W1 = jax.random.normal(ks[2], (E, F, D), jnp.float32) * 0.02
        b1 = jnp.zeros((E, F), jnp.float32)
        W2 = jax.random.normal(ks[3], (E, D, F), jnp.float32) * 0.02
        b2 = jnp.zeros((E, D), jnp.float32)
        return {'x': x, 'centroids': centroids, 'gamma': gamma, 'beta': beta, 'W1': W1, 'b1': b1, 'W2': W2, 'b2': b2}
    _L0_ffn_in = _L0_ffn_setup()
    _d = {'L0_attn_resid': _L0_attn_in['resid'], 'L0_attn_norm_w': _L0_attn_in['norm_w'], 'L0_attn_skip_w': _L0_attn_in['skip_w'], 'L0_attn_in_w': _L0_attn_in['in_w'], 'L0_attn_conv_w': _L0_attn_in['conv_w'], 'L0_attn_conv_b': _L0_attn_in['conv_b'], 'L0_attn_wd1': _L0_attn_in['wd1'], 'L0_attn_wd2': _L0_attn_in['wd2'], 'L0_attn_wd2_b': _L0_attn_in['wd2_b'], 'L0_attn_wb': _L0_attn_in['wb'], 'L0_attn_wc': _L0_attn_in['wc'], 'L0_attn_A_log': _L0_attn_in['A_log'], 'L0_attn_W_D': _L0_attn_in['W_D'], 'L0_attn_out_w': _L0_attn_in['out_w'], 'L0_ffn_centroids': _L0_ffn_in['centroids'], 'L0_ffn_gamma': _L0_ffn_in['gamma'], 'L0_ffn_beta': _L0_ffn_in['beta'], 'L0_ffn_W1': _L0_ffn_in['W1'], 'L0_ffn_b1': _L0_ffn_in['b1'], 'L0_ffn_W2': _L0_ffn_in['W2'], 'L0_ffn_b2': _L0_ffn_in['b2']}
    _x0 = _d['L0_attn_resid']
    _d['L0_attn_resid'] = jax.random.normal(jax.random.fold_in(jax.random.key(seed), 1), (4, 1024, 128), dtype=_x0.dtype)
    del _x0
    return _d

def reference(L0_attn_resid, L0_attn_norm_w, L0_attn_skip_w, L0_attn_in_w, L0_attn_conv_w, L0_attn_conv_b, L0_attn_wd1, L0_attn_wd2, L0_attn_wd2_b, L0_attn_wb, L0_attn_wc, L0_attn_A_log, L0_attn_W_D, L0_attn_out_w, L0_ffn_centroids, L0_ffn_gamma, L0_ffn_beta, L0_ffn_W1, L0_ffn_b1, L0_ffn_W2, L0_ffn_b2):

    def _L0_attn_ref(resid, norm_w, skip_w, in_w, conv_w, conv_b, wd1, wd2, wd2_b, wb, wc, A_log, W_D, out_w):
        import jax, jax.numpy as jnp
        import numpy as np
        D_MODEL, D_INNER, D_STATE, DT_RANK, D_CONV = (128, 256, 16, 64, 4)
        B, L = (2, 256)

        def _rmsnorm(x, w, eps=1e-05):
            return x * jax.lax.rsqrt(jnp.mean(x * x, axis=-1, keepdims=True) + eps) * w

        def _causal_depthwise_conv(x, conv_w, conv_b):
            K = conv_w.shape[1]
            xp = jnp.pad(x, ((0, 0), (K - 1, 0), (0, 0)))
            Lx = x.shape[1]
            out = conv_b
            for k in range(K):
                out = out + xp[:, k:k + Lx, :] * conv_w[:, k]
            return out

        def _selective_scan(x, delta, Bm, Cm, A):
            h0 = jnp.zeros((x.shape[0], A.shape[0], A.shape[1]), x.dtype)

            def step(h, inp):
                xt, dt, bt, ct = inp
                A_bar = jnp.exp(dt[..., None] * A)
                h = A_bar * h + (dt * xt)[..., None] * bt[:, None, :]
                y = jnp.einsum('ben,bn->be', h, ct)
                return (h, y)
            xs = tuple((jnp.swapaxes(a, 0, 1) for a in (x, delta, Bm, Cm)))
            _, ys = jax.lax.scan(step, h0, xs)
            return jnp.swapaxes(ys, 0, 1)
        x = _rmsnorm(resid, norm_w)
        skip = x @ skip_w.T
        x = x @ in_w.T
        x = _causal_depthwise_conv(x, conv_w, conv_b)
        x = jax.nn.silu(x)
        A = -jnp.exp(A_log)
        delta = jax.nn.softplus(x @ wd1.T @ wd2.T + wd2_b)
        Bm = x @ wb.T
        Cm = x @ wc.T
        y = _selective_scan(x, delta, Bm, Cm, A)
        y = y + x * W_D
        y = y * jax.nn.silu(skip)
        y = y @ out_w.T
        return resid + y

    def _L0_ffn_ref(x, centroids, gamma, beta, W1, b1, W2, b2):
        import jax, jax.numpy as jnp
        import numpy as np
        B, S, D, F, E = (1, 128, 128, 512, 8)
        EPS = 1e-05

        def _sublayer(xs, g, b, W1e, b1e, W2e, b2e):
            mu = jnp.mean(xs, axis=-1, keepdims=True)
            var = jnp.mean(jnp.square(xs - mu), axis=-1, keepdims=True)
            h = (xs - mu) * jax.lax.rsqrt(var + EPS) * g + b
            return xs + jax.nn.relu(h @ W1e.T + b1e) @ W2e.T + b2e
        feats = x.reshape(-1, x.shape[-1])
        scores = jax.lax.stop_gradient(feats @ centroids.T)
        expert = jnp.argmax(scores, axis=1)
        onehot = jax.nn.one_hot(expert, E, dtype=feats.dtype)
        alpha = jax.nn.sigmoid(jnp.sum(feats * centroids[expert], axis=-1, keepdims=True))
        ys = jax.vmap(_sublayer, in_axes=(None, 0, 0, 0, 0, 0, 0))(feats, gamma, beta, W1, b1, W2, b2)
        y = jnp.einsum('te,etd->td', onehot, ys)
        out = alpha * y + (1.0 - alpha) * feats
        return out.reshape(x.shape)
    x = L0_attn_resid
    x = x + 0.5 * _L0_ffn_ref(_layernorm(x, axis=-1), L0_ffn_centroids, L0_ffn_gamma, L0_ffn_beta, L0_ffn_W1, L0_ffn_b1, L0_ffn_W2, L0_ffn_b2)
    x = x + _L0_attn_ref(_layernorm(x, axis=-1), L0_attn_norm_w, L0_attn_skip_w, L0_attn_in_w, L0_attn_conv_w, L0_attn_conv_b, L0_attn_wd1, L0_attn_wd2, L0_attn_wd2_b, L0_attn_wb, L0_attn_wc, L0_attn_A_log, L0_attn_W_D, L0_attn_out_w)
    x = x + 0.5 * _L0_ffn_ref(_layernorm(x, axis=-1), L0_ffn_centroids, L0_ffn_gamma, L0_ffn_beta, L0_ffn_W1, L0_ffn_b1, L0_ffn_W2, L0_ffn_b2)
    return x

_drawn_inputs = setup_inputs


def setup_inputs(seed=0):
    import zlib

    import numpy as np

    out = dict(_drawn_inputs(seed))
    spreads = {'L0_attn_norm_w': (1.0, 0.2),
     'L0_attn_conv_b': (0.0, 0.1),
     'L0_attn_wd2_b': (0.0, 0.581),
     'L0_attn_W_D': (1.0, 0.2),
     'L0_ffn_gamma': (1.0, 0.6),
     'L0_ffn_beta': (0.0, 2.0),
     'L0_ffn_b1': (0.0, 0.625),
     'L0_ffn_b2': (0.0, 0.1)}
    factors = {}
    for name, (base, spread) in spreads.items():
        noise = np.random.default_rng([zlib.crc32(name.encode()), seed]).standard_normal(out[name].shape)
        drawn = base * np.exp(spread * noise) if base else spread * noise
        out[name] = jnp.asarray(drawn.astype(out[name].dtype))
    for name, factor in factors.items():
        out[name] = (out[name] * factor).astype(out[name].dtype)
    return out
```

```python
from contextlib import ExitStack

import concourse.bass as bass
from concourse import mybir

ALU = mybir.AluOpType
ACT = mybir.ActivationFunctionType
F32 = mybir.dt.float32
BF16 = mybir.dt.bfloat16
I32 = mybir.dt.int32
AX = mybir.AxisListType.X

P = 128
D = 128
E = 8
F = 512
FC = F // P
TOK = 4096
NT = TOK // P
ST = NT + E - 1
GT = 3
NG = ST // GT
XR = 4
YR = 4
PK = F + FC * D + FC + 2 + D
O_W2, O_B1 = F, F + FC * D
O_G, O_B, O_B2 = O_B1 + FC, O_B1 + FC + 1, O_B1 + FC + 2
EPS = 1e-5

H2 = 2
NS = 16
R = 64
TAPS = 4
C = 512
CT = C // P
NCH = TOK // C
HIST = 4
assert ST % GT == 0 and NT % 4 == 0


def lin(i, k, c):
    if isinstance(i, tuple):
        reg, a, b = i
        return reg * (a * k) + (b * k + c)
    return k * i + c


def wait(eng, sem, value):
    if not isinstance(value, int) or value > 0:
        eng.wait_ge(sem, value)


def at(i, size, off=0, n=None):
    n = size if n is None else n
    v = lin(i, size, off)
    return slice(v, v + n) if isinstance(v, int) else bass.ds(v, n)


def build(nc, a, out):
    with ExitStack() as ctx:
        def sb(name, shape, dt=F32):
            return ctx.enter_context(nc.sbuf_tensor(name, shape, dt))

        def ps(name, shape):
            return ctx.enter_context(nc.psum_tensor(name, shape, F32))

        def sem(name):
            return ctx.enter_context(nc.semaphore(name))

        X = sb("X", [P, NT, D])
        wall = sb("wall", [P, E, PK])
        centT = sb("centT", [D, E])
        DA, HB, HC = 4 * H2 * C, 2 * H2 * C, 4 * H2 * C
        XHN, WCN, YSN = NT * D, 3 * PK, YR * GT * D
        region = sb("region", [P, max(DA + HB + HC, XHN + WCN + YSN)])
        xh = region[:, 0:XHN].rearrange("p (t d) -> p t d", d=D)
        wcur = region[:, XHN:XHN + WCN].rearrange("p (r w) -> p r w", w=PK)
        ys = region[:, XHN + WCN:XHN + WCN + YSN].rearrange("p (t d) -> p t d", d=D)
        dA = region[:, 0:DA].rearrange("p (r h c) -> p r h c", r=4, h=H2)
        hb = region[:, DA:DA + HB].rearrange("p (r h c) -> p r h c", r=2, h=H2)
        hc = region[:, DA + HB:DA + HB + HC].rearrange("p (r h c) -> p r h c", r=4, h=H2)
        xs = sb("xs", [P, XR * GT, D])
        gath = xs
        ftT = sb("ftT", [D, 2, C])
        xsT = sb("xsT", [D, 3, P])
        hT = sb("hT", [P, 3, FC, P])
        stat = sb("stat", [P, NT, 6])
        mom = sb("mom", [P, 4, NT])
        lnin = sb("lnin", [P, 2, NT])
        lnl = sb("lnl", [P, 2, NT])
        rst = sb("rst", [P, 2, NT])
        inv = sb("inv", [P, NT])
        r12 = sb("r12", [P, NT])
        xa = sb("xa", [P, NT])
        xb = sb("xb", [P, NT])
        score = sb("score", [P, NT, E])
        tmpA = sb("tmpA", [P, NT * E])
        tmpB = sb("tmpB", [P, NT * E])
        tot = sb("tot", [P, NT * E])
        oh = sb("oh", [P, E, NT], BF16)
        mx = sb("mx", [P, NT])
        best = sb("best", [P, NT])
        zal = sb("zal", [P, NT])
        eal = sb("eal", [P, NT])
        half_alpha = sb("half_alpha", [P, NT])
        slot_f = sb("slot_f", [P, NT])
        slot = sb("slot", [P, NT], I32)
        small = sb("small", [P, 8, E])
        nti = sb("nti", [P, 2, E], I32)
        cmp = sb("cmp", [P, ST, E])
        texf = sb("texf", [P, ST])
        tex = sb("tex", [P, ST], I32)
        ident = sb("ident", [P, P])
        upper = sb("upper", [P, P], BF16)
        ones_b = sb("ones_b", [P, P], BF16)
        ones_f = sb("ones_f", [P, NT * E])
        desc = sb("desc", [P, E])
        jcon = sb("jcon", [P, ST])
        rowsel = sb("rowsel", [P, 32])
        sel = sb("sel", [P, 32, P], BF16)
        par = sb("par", [P, 2 * NS + 7])
        alog = par[:, 0:2 * NS]
        conv_b = par[:, 2 * NS:2 * NS + 2]
        wd2_b = par[:, 2 * NS + 2:2 * NS + 4]
        w_D = par[:, 2 * NS + 4:2 * NS + 6]
        norm_w = par[:, 2 * NS + 6:2 * NS + 7]
        expA = sb("expA", [P, 2 * NS])
        negA = sb("negA", [P, 2 * NS])
        in_wT = sb("in_wT", [D, H2 * P])
        skip_wT = sb("skip_wT", [D, H2 * P])
        cw = sb("cw", [P, TAPS, H2 * P])
        wd1T = sb("wd1T", [P, H2, R])
        wd2T = sb("wd2T", [R, H2 * P])
        wbcT = sb("wbcT", [P, H2, P])
        out_wT = sb("out_wT", [P, H2, D])
        xr = sb("xr", [P, CT, D])
        xrT = sb("xrT", [D, 2, HIST + C])
        cst = sb("cst", [P, CT, 6])
        cmom = sb("cmom", [P, 4, CT])
        csm = sb("csm", [P, 10, CT])
        xc = sb("xc", [P, 2, H2, C])
        sg = sb("sg", [P, 2, H2, C])
        dt = sb("dt", [P, 2, H2, C])
        u = sb("u", [P, 2, H2, C])
        dtr = sb("dtr", [R, C])
        bcs = sb("bcs", [P, 2, C], BF16)
        bcr = sb("bcr", [P, C])
        sp_t = sb("sp_t", [P, H2, C])
        bu = sb("bu", [P, 2, H2, C])
        cs = sb("cs", [P, 2, C])
        yg = sb("yg", [P, H2, C])
        carry = sb("carry", [P, NS, H2])

        bank = [ps(f"bank{i}", [P, 512]) for i in range(8)]
        tr_ps = [bank[0], bank[1]]
        sc_ps = bank[2][:, 0:NT * E].rearrange("p (t e) -> p t e", e=E)
        rank_ps, tot_ps = bank[3][:, 0:NT * E], bank[3][:, NT * E:2 * NT * E]
        xt_ps = [bank[4][:, 0:P], bank[3][:, 0:P]]
        ha_ps = [bank[5], bank[7]]
        hd_ps = [bank[6], bank[2]]
        y_ps = [bank[0][:, 0:D], bank[1][:, 0:D]]
        w_ps = [bank[0], bank[1]]
        b_ps = [bank[2], bank[3]]
        c_ps = [bank[4], bank[5]]
        acc_ps = [bank[6], bank[7]]

        rows_d = nc.dram_tensor("sorted_rows", [ST * P, D], F32, kind="Internal").ap()
        res_d = nc.dram_tensor("sorted_results", [ST * P, D], F32, kind="Internal").ap()
        rows_v = rows_d.rearrange("(t p) d -> p t d", p=P)
        res_v = res_d.rearrange("(t p) d -> p t d", p=P)
        x_v = a["x"].rearrange("(t p) d -> p t d", p=P)
        out_v = out.rearrange("(t p) d -> p t d", p=P)

        s_x = [sem(f"x_loaded{i}") for i in range(NT // 4)]
        s_par = sem("params_loaded")
        s_w = sem("expert_weights_loaded")
        s_cent = sem("centroids_loaded")
        s_zero = sem("xs_zeroed")
        s_zst = sem("rows_zeroed")
        s_pc = sem("pool_consts")
        s_dc = sem("dve_consts")
        s_ea = sem("exp_a_log")
        own = sem("dve_chain")
        s_lnin = sem("variances_ready")
        s_lnl = sem("logs_ready")
        s_rst = sem("rstd_ready")
        s_xh = sem("normed_ready")
        s_trA = sem("normed_transposed")
        s_ftT = sem("normedT_copied")
        s_sc = sem("scores_done")
        s_z = sem("alpha_arg_ready")
        s_ez = sem("alpha_exp_done")
        s_oh = sem("onehot_ready")
        s_rank = sem("ranks_done")
        s_slot = sem("slots_ready")
        s_tex = sem("tile_experts_ready")
        s_scat = sem("rows_scattered")
        s_xs = [sem(f"sorted_loaded{i}") for i in range(NG)]
        s_xt = sem("sorted_transposed")
        s_xsT = sem("sortedT_copied")
        s_wc = sem("weights_current")
        s_h = sem("hidden_done")
        s_ra = sem("relu_act_done")
        s_rd = sem("relu_dve_done")
        s_y = sem("result_done")
        s_ys = sem("result_copied")
        s_yst = sem("results_stored")
        s_g = [sem(f"gathered{i}") for i in range(XR * GT)]
        s_x1 = sem("ffn_residual_added")
        s_out = sem("output_stored")
        s_cln = sem("m_variances_ready")
        s_cl = sem("m_logs_ready")
        s_cr = sem("m_rstd_ready")
        s_xr = sem("m_normed_ready")
        s_u0 = sem("m_transposed")
        s_xrT = sem("m_normedT_copied")
        s_hist = sem("m_history_copied")
        s_conv = sem("m_conv_done")
        s_skip = sem("m_skip_done")
        s_xc = sem("m_x_ready")
        s_sg = sem("m_gate_ready")
        s_dtr = sem("m_dtrank_done")
        s_dtc = sem("m_dtrank_copied")
        s_bc = sem("m_bc_done")
        s_hi = sem("m_bc_high_part")
        s_split = sem("m_bc_split")
        s_zz = sem("m_dtarg_done")
        s_abs = sem("m_dtarg_abs")
        s_ex = sem("m_softplus_exp")
        s_sp = sem("m_softplus_log")
        s_rz = sem("m_dtarg_relu")
        s_dt = sem("m_dt_ready")
        s_u = sem("m_dtx_ready")
        s_b = sem("m_b_broadcast")
        s_c = sem("m_c_broadcast")
        s_cs = sem("m_c_copied")
        s_dA = sem("m_decay_ready")
        s_bu = sem("m_dtxb_ready")
        s_scan = sem("m_scanned")
        s_car = sem("m_carry_saved")
        s_hc = sem("m_hc_ready")
        s_acc = sem("m_summed")
        s_yg = sem("m_y_read")
        s_gate = sem("m_gated")
        s_o = sem("m_projected")
        s_x2 = sem("m_residual_added")
        s_own2 = sem("m_norm_chain")
        s_own3 = sem("m_split_chain")

        block = ctx.enter_context(nc.Block())

        @block.sync
        def _(sp):
            for g in range(NT // 4):
                sp.dma_start(X[:, 4 * g:4 * g + 4, :], x_v[:, 4 * g:4 * g + 4, :]).then_inc(s_x[g], 16)
            sp.dma_start(centT[:, :], a["centT"]).then_inc(s_cent, 16)
            sp.dma_start(wall[:, :, 0:O_B2], a["experts"]).then_inc(s_w, 16)
            sp.dma_start(wall[:, :, O_B2:PK], a["b2"].partition_broadcast(P)).then_inc(s_w, 16)
            sp.wait_ge(s_zero, 1)
            for t in range(0, ST, XR * GT):
                n = min(XR * GT, ST - t)
                sp.dma_start(rows_v[:, t:t + n, :], xs[:, 0:n, :]).then_inc(s_zst, 16)
            for dst, src in ((par, "par"), (in_wT, "in_wT"), (skip_wT, "skip_wT"), (wd2T, "wd2T")):
                sp.dma_start(dst[:, :], a[src]).then_inc(s_par, 16)
            for dst, src in ((wd1T, "wd1T"), (out_wT, "out_wT")):
                sp.dma_start(dst[:, :, :], a[src]).then_inc(s_par, 16)
            sp.dma_start(cw[:, :, :], a["conv_wT"].partition_broadcast(P)).then_inc(s_par, 16)
            sp.wait_ge(s_dc, 1)
            for c0 in (0, 64, 96):
                sp.dma_start(wbcT[:, :, c0:c0 + 32], a["wbcT"]).then_inc(s_par, 16)

            for f in range(2):
                sp.wait_ge(s_scat, 16 * NT * (f + 1))

                def load(g):
                    if g >= XR:
                        sp.wait_ge(s_xt, ST * f + GT * (g - XR + 1))
                    r = g % XR
                    sp.dma_start(xs[:, GT * r:GT * r + GT, :],
                                 rows_v[:, GT * g:GT * g + GT, :]).then_inc(s_xs[g], 16)

                for g in range(XR):
                    load(g)
                for g in range(NG):
                    sp.wait_ge(s_ys, ST * f + GT * (g + 1))
                    r = g % YR
                    sp.dma_start(res_v[:, GT * g:GT * g + GT, :],
                                 ys[:, GT * r:GT * r + GT, :]).then_inc(s_yst, 16)
                    if g + XR < NG:
                        load(g + XR)
            for g in range(NT // 4):
                sp.wait_ge(s_x1, NT + 4 * (g + 1))
                sp.dma_start(out_v[:, 4 * g:4 * g + 4, :], X[:, 4 * g:4 * g + 4, :]).then_inc(s_out, 16)
            sp.wait_ge(s_out, 16 * NT // 4)

        @block.gpsimd
        def _(pool):
            pool.memset(ident[:, :], 0.0).then_inc(s_pc, 1)
            pool.memset(upper[:, :], 0.0).then_inc(s_pc, 1)
            pool.memset(ones_b[:, :], 1.0).then_inc(s_pc, 1)
            pool.memset(ones_f[:, :], 1.0).then_inc(s_pc, 1)
            pool.memset(xrT[:, 0, 0:HIST], 0.0).then_inc(s_pc, 1)
            pool.wait_ge(s_pc, 5)
            pool.affine_select(out=ident[:, :], in_=ident[:, :], compare_op=ALU.not_equal, fill=1.0,
                               base=0, pattern=[[-1, P]], channel_multiplier=1).then_inc(s_pc, 1)
            pool.affine_select(out=upper[:, :], in_=upper[:, :], compare_op=ALU.is_ge, fill=1.0,
                               base=0, pattern=[[-1, P]], channel_multiplier=1).then_inc(s_pc, 1)
            pool.iota(desc[:, :], pattern=[[-1, E]], base=E, channel_multiplier=0,
                      allow_small_or_imprecise_dtypes=True).then_inc(s_pc, 1)
            pool.iota(jcon[:, :], pattern=[[1, ST]], base=0, channel_multiplier=0,
                      allow_small_or_imprecise_dtypes=True).then_inc(s_pc, 1)

            def scatter(f):
                pool.wait_ge(s_slot, f + 1)
                if f == 0:
                    pool.wait_ge(s_zst, 16 * -(-ST // (XR * GT)))
                pool.wait_ge(s_xh, NT * (f + 1))
                for t in range(NT):
                    pool.indirect_dma_start(rows_d, bass.IndirectOffsetOnAxis(ap=slot[:, t:t + 1], axis=0),
                                            xh[:, t, :], None).then_inc(s_scat, 16)

            def gather(f):
                pool.wait_ge(s_yst, 16 * NG * (f + 1))
                for t in range(NT):
                    r = t % (XR * GT)
                    if t >= XR * GT:
                        pool.wait_ge(s_x1, NT * f + t - XR * GT + 1)
                    pool.indirect_dma_start(gath[:, r, :], None, res_d,
                                            bass.IndirectOffsetOnAxis(ap=slot[:, t:t + 1], axis=0)
                                            ).then_inc(s_g[r], 16)

            def dtx(p, par_):
                wait(pool, s_dt, lin(p, 2, 2))
                wait(pool, s_xc, lin(p, 2, 2))
                pool.tensor_tensor(u[:, par_], dt[:, par_], xc[:, par_], ALU.mult).then_inc(s_u, 1)

            def gate(o, par_):
                wait(pool, s_yg, lin(o, 2, 2))
                wait(pool, s_sg, lin(o, 2, 2))
                pool.tensor_tensor(yg[:, :, :], yg[:, :, :], sg[:, par_], ALU.mult).then_inc(s_gate, 1)

            def window(g, par_, post, prep):
                for n in range(NS):
                    wait(pool, s_scan, lin(g, 2 * NS, 2 * n + 2))
                    wait(pool, s_cs, lin(g, NS, n + 1))
                    wait(pool, s_acc, lin(g, 2 * NS, 2 * (n - 4) + 2))
                    pool.tensor_tensor(hc[:, n % 4], hb[:, n % 2],
                                       cs[:, n % 2].unsqueeze(1).broadcast_to([P, H2, C]),
                                       ALU.mult).then_inc(s_hc, 1)
                    if n == 2 and post is not None:
                        gate(post, 1 - par_)
                    if n == 12 and prep is not None:
                        dtx(prep, 1 - par_)

            scatter(0)
            gather(0)
            dtx(0, 0)
            window(0, 0, None, 1)
            with pool.Fori(0, (NCH - 2) // 2) as i:
                window((i, 2, 1), 1, (i, 2, 0), (i, 2, 2))
                window((i, 2, 2), 0, (i, 2, 1), (i, 2, 3))
            window(NCH - 1, 1, NCH - 2, None)
            gate(NCH - 1, 1)
            scatter(1)
            gather(1)

        @block.scalar
        def _(act):
            act.wait_ge(s_par, 16 * 10)
            nc.scalar.preload_act_table_set("natural_log_exp_and_others")
            nc.scalar.activation(expA[:, :], alog, ACT.Exp).then_inc(s_ea, 1)

            def ffn(f):
                act.wait_ge(s_lnin, f + 1)
                nc.scalar.activation(lnl[:, :, :], lnin[:, :, :], ACT.Ln).then_inc(s_lnl, 1)
                act.wait_ge(s_lnl, f + 1)
                nc.scalar.activation(rst[:, :, :], lnl[:, :, :], ACT.Exp, scale=-0.5).then_inc(s_rst, 1)
                for g in range(NT // 4):
                    act.wait_ge(s_trA, NT // 4 * f + g + 1)
                    if g >= 2:
                        act.wait_ge(s_sc, NT // 4 * f + g - 1)
                    nc.scalar.activation(ftT[:, g % 2], tr_ps[g % 2][:, :], ACT.Copy).then_inc(s_ftT, 1)
                act.wait_ge(s_z, f + 1)
                nc.scalar.activation(eal[:, :], zal[:, :], ACT.Exp, scale=-1.0).then_inc(s_ez, 1)

                def tile(j, s):
                    wait(act, s_xt, lin(j, 1, ST * f + 1))
                    wait(act, s_wc, lin(j, 1, ST * f + 1))
                    wait(act, s_h, lin(j, 1, ST * f - 2))
                    nc.scalar.activation(xsT[:, s % GT], xt_ps[s % 2], ACT.Identity,
                                         scale=wcur[:, s % GT, O_G:O_G + 1],
                                         bias=wcur[:, s % GT, O_B:O_B + 1]).then_inc(s_xsT, 1)

                def relu(j, s):
                    wait(act, s_h, lin(j, 1, ST * f + 1))
                    wait(act, s_y, lin(j, 1, ST * f - 2))
                    for c in (0, 1):
                        nc.scalar.activation(hT[:, s % GT, c], ha_ps[s % 2][:, P * c:P * c + P], ACT.Relu,
                                             bias=wcur[:, s % GT, O_B1 + c:O_B1 + c + 1]).then_inc(s_ra, 1)

                U = 2 * GT

                tile(0, 0)
                for j in range(U):
                    tile(j + 1, j + 1)
                    relu(j, j)
                with act.Fori(1, ST // U) as i:
                    for s in range(U):
                        tile((i, U, s + 1), s + 1)
                        relu((i, U, s), s)
                for j in range(ST // U * U, ST):
                    if j + 1 < ST:
                        tile(j + 1, j + 1)
                    relu(j, j)

            def prep_norm(p):
                wait(act, s_cln, lin(p, 1, 1))
                nc.scalar.activation(csm[:, 2:4, :], csm[:, 0:2, :], ACT.Ln).then_inc(s_cl, 1)
                wait(act, s_cl, lin(p, 1, 1))
                nc.scalar.activation(csm[:, 4:6, :], csm[:, 2:4, :], ACT.Exp, scale=-0.5).then_inc(s_cr, 1)

            def prep_xrT(p, q):
                wait(act, s_u0, lin(p, 1, 1))
                nc.scalar.activation(xrT[:, q, HIST:HIST + C], w_ps[0][:, :], ACT.Copy).then_inc(s_xrT, 1)
                if q == 1:
                    nc.scalar.activation(xrT[:, 1, 0:HIST], xrT[:, 0, C:C + HIST], ACT.Copy).then_inc(s_hist, 1)

            def prep_silu(p, q):
                for h in range(H2):
                    wait(act, s_conv, lin(p, 2, h + 1))
                    wait(act, s_yg, lin(p, 2, -2))
                    nc.scalar.activation(xc[:, q, h], w_ps[1 - h][:, :], ACT.Silu,
                                         bias=conv_b[:, h:h + 1]).then_inc(s_xc, 1)
                for h in range(H2):
                    wait(act, s_skip, lin(p, 2, h + 1))
                    wait(act, s_gate, lin(p, 1, -1))
                    nc.scalar.activation(sg[:, q, h], w_ps[1 - h][:, :], ACT.Silu).then_inc(s_sg, 1)

            def prep_dtr(p):
                wait(act, s_dtr, lin(p, 1, 1))
                wait(act, s_zz, lin(p, 2, 0))
                nc.scalar.activation(dtr[:, :], w_ps[0][0:R, :], ACT.Copy).then_inc(s_dtc, 1)

            def prep_bc(p, q):
                wait(act, s_bc, lin(p, 1, 1))
                nc.scalar.activation(bcs[:, q], w_ps[1][:, :], ACT.Copy).then_inc(s_hi, 1)

            def prep_softplus(p):
                for h in range(H2):
                    wait(act, s_zz, lin(p, 2, h + 1))
                    wait(act, s_dt, lin(p, 2, h - 1))
                    nc.scalar.activation(sp_t[:, h], w_ps[h][:, :], ACT.Abs,
                                         bias=wd2_b[:, h:h + 1]).then_inc(s_abs, 1)
                for h in range(H2):
                    wait(act, s_abs, lin(p, 2, h + 1))
                    nc.scalar.activation(sp_t[:, h], sp_t[:, h], ACT.Exp, scale=-1.0).then_inc(s_ex, 1)
                for h in range(H2):
                    wait(act, s_ex, lin(p, 2, h + 1))
                    nc.scalar.activation(sp_t[:, h], sp_t[:, h], ACT.Ln, bias=1.0).then_inc(s_sp, 1)

            def decay(g, q, n):
                if n == 0:
                    wait(act, s_dt, lin(g, 2, 2))
                wait(act, s_scan, lin(g, 2 * NS, 2 * (n - 4) + 2))
                for h in range(H2):
                    nc.scalar.activation(dA[:, n % 4, h], dt[:, q, h], ACT.Exp,
                                         scale=negA[:, h * NS + n:h * NS + n + 1]).then_inc(s_dA, 1)

            def copy_c(g, n):
                wait(act, s_c, lin(g, NS, n + 1))
                wait(act, s_hc, lin(g, NS, n - 1))
                nc.scalar.activation(cs[:, n % 2], c_ps[n % 2][:, :], ACT.Copy).then_inc(s_cs, 1)

            def window(g, q, nxt, prep):
                for n in range(NS):
                    if n + 2 < NS:
                        decay(g, q, n + 2)
                    elif nxt is not None:
                        decay(nxt, 1 - q, n + 2 - NS)
                    if n + 1 < NS:
                        copy_c(g, n + 1)
                    elif nxt is not None:
                        copy_c(nxt, 0)
                    if prep is not None:
                        if n == 0:
                            prep_norm(prep)
                        if n == 2:
                            prep_xrT(prep, 1 - q)
                        if n == 5:
                            prep_silu(prep, 1 - q)
                        if n == 7:
                            prep_dtr(prep)
                        if n == 8:
                            prep_bc(prep, 1 - q)
                        if n == 9:
                            prep_softplus(prep)

            ffn(0)
            act.wait_ge(s_dc, 11)
            prep_norm(0)
            prep_xrT(0, 0)
            prep_silu(0, 0)
            prep_dtr(0)
            prep_bc(0, 0)
            prep_softplus(0)
            decay(0, 0, 0)
            decay(0, 0, 1)
            copy_c(0, 0)
            window(0, 0, 1, 1)
            with act.Fori(0, (NCH - 2) // 2) as i:
                window((i, 2, 1), 1, (i, 2, 2), (i, 2, 2))
                window((i, 2, 2), 0, (i, 2, 3), (i, 2, 3))
            window(NCH - 1, 1, None, None)
            ffn(1)

        @block.tensor
        def _(pe):
            mm = nc.tensor.matmul

            def ffn(f):
                pe.wait_ge(s_pc, 9)
                if f == 0:
                    pe.wait_ge(s_cent, 16)

                def scores(g):
                    pe.wait_ge(s_ftT, NT // 4 * f + g + 1)
                    for k in range(4):
                        last = mm(sc_ps[:, 4 * g + k, :], ftT[:, g % 2, P * k:P * k + P], centT[:, :],
                                  start=True, stop=True)
                    last.then_inc(s_sc, 1)

                for g in range(NT // 4):
                    pe.wait_ge(s_xh, NT * f + 4 * (g + 1))
                    if g >= 2:
                        pe.wait_ge(s_ftT, NT // 4 * f + g - 1)
                    for k in range(4):
                        last = nc.tensor.transpose(tr_ps[g % 2][:, P * k:P * k + P], xh[:, 4 * g + k, :], ident[:, :])
                    last.then_inc(s_trA, 1)
                    if g >= 1:
                        scores(g - 1)
                scores(NT // 4 - 1)
                pe.wait_ge(s_oh, f + 1)
                oh_v = oh[:, :, :].rearrange("p e t -> p (e t)")
                mm(rank_ps, upper[:, :], oh_v, start=True, stop=True)
                mm(tot_ps, ones_b[:, :], oh_v, start=True, stop=True).then_inc(s_rank, 1)

                def transpose(j):
                    if j % GT == 0:
                        pe.wait_ge(s_xs[j // GT], 16 * (f + 1))
                    wait(pe, s_xsT, ST * f + j - 1)
                    nc.tensor.transpose(xt_ps[j % 2], xs[:, j % (XR * GT), :], ident[:, :]).then_inc(s_xt, 1)

                def hidden(j):
                    pe.wait_ge(s_wc, ST * f + j + 1)
                    pe.wait_ge(s_xsT, ST * f + j + 1)
                    wait(pe, s_ra, 2 * (ST * f + j) - 2)
                    wait(pe, s_rd, 2 * (ST * f + j) - 2)
                    for c in range(FC):
                        to = (ha_ps if c < 2 else hd_ps)[j % 2]
                        last = mm(to[:, P * (c % 2):P * (c % 2) + P], wcur[:, j % GT, P * c:P * c + P],
                                  xsT[:, j % GT], start=True, stop=True)
                    last.then_inc(s_h, 1)

                def result(j):
                    pe.wait_ge(s_ra, 2 * (ST * f + j) + 2)
                    pe.wait_ge(s_rd, 2 * (ST * f + j) + 2)
                    wait(pe, s_ys, ST * f + j - 1)
                    for c in range(FC):
                        last = mm(y_ps[j % 2], hT[:, j % GT, c],
                                  wcur[:, j % GT, O_W2 + D * c:O_W2 + D * c + D],
                                  start=(c == 0), stop=(c == FC - 1))
                    last.then_inc(s_y, 1)

                transpose(0)
                for j in range(ST):
                    if j + 1 < ST:
                        transpose(j + 1)
                    hidden(j)
                    if j >= 1:
                        result(j - 1)
                result(ST - 1)

            def p_transpose(p):
                wait(pe, s_xr, lin(p, 1, 1))
                wait(pe, s_rz, lin(p, 2, -1))
                wait(pe, s_abs, lin(p, 2, -1))
                for k in range(CT):
                    last = nc.tensor.transpose(w_ps[0][:, P * k:P * k + P], xr[:, k, :], ident[:, :])
                last.then_inc(s_u0, 1)

            def p_conv(p, q, h):
                wait(pe, s_xrT, lin(p, 1, 1))
                if q == 1:
                    pe.wait_ge(s_hist, (p + 1) // 2 if isinstance(p, int) else p[0] * (p[1] // 2) + (p[2] + 1) // 2)
                if h == 0:
                    wait(pe, s_rz, lin(p, 2, 0))
                    wait(pe, s_abs, lin(p, 2, 0))
                for k in range(TAPS):
                    o = HIST - (TAPS - 1) + k
                    last = mm(w_ps[1 - h][:, :], cw[:, k, P * h:P * h + P], xrT[:, q, o:o + C],
                              start=(k == 0), stop=(k == TAPS - 1))
                last.then_inc(s_conv, 1)

            def p_skip(p, q, h):
                wait(pe, s_xc, lin(p, 2, h + 1))
                mm(w_ps[1 - h][:, :], skip_wT[:, P * h:P * h + P], xrT[:, q, HIST:HIST + C],
                   start=True, stop=True).then_inc(s_skip, 1)

            def p_dtr(p, q):
                wait(pe, s_sg, lin(p, 2, 2))
                for h in range(H2):
                    last = mm(w_ps[0][0:R, :], wd1T[:, h], xc[:, q, h], start=(h == 0), stop=(h == 1))
                last.then_inc(s_dtr, 1)

            def p_bc(p, q, post):
                wait(pe, s_sg, lin(p, 2, 1))
                if post is not None:
                    wait(pe, s_x2, lin(post, 1, 1))
                for h in range(H2):
                    last = mm(w_ps[1][:, :], wbcT[:, h], xc[:, q, h], start=(h == 0), stop=(h == 1))
                last.then_inc(s_bc, 1)

            def p_z(p):
                wait(pe, s_dtc, lin(p, 1, 1))
                mm(w_ps[0][:, :], wd2T[:, 0:P], dtr[:, :], start=True, stop=True).then_inc(s_zz, 1)
                wait(pe, s_split, lin(p, 1, 1))
                mm(w_ps[1][:, :], wd2T[:, P:2 * P], dtr[:, :], start=True, stop=True).then_inc(s_zz, 1)

            def bcast(g, q, n):
                if n == 0:
                    wait(pe, s_split, lin(g, 1, 1))
                wait(pe, s_bu, lin(g, NS, n - 1))
                mm(b_ps[n % 2][:, :], sel[:, n], bcs[:, q], start=True, stop=True).then_inc(s_b, 1)
                wait(pe, s_cs, lin(g, NS, n - 1))
                mm(c_ps[n % 2][:, :], sel[:, NS + n], bcs[:, q], start=True, stop=True).then_inc(s_c, 1)

            def summed(g, n):
                wait(pe, s_hc, lin(g, NS, n + 1))
                if n == 0:
                    wait(pe, s_yg, lin(g, 2, 0))
                for h in range(H2):
                    mm(acc_ps[h][:, :], ident[:, :], hc[:, n % 4, h], start=(n == 0), stop=(n == NS - 1),
                       ).then_inc(s_acc, 1)

            def project(o):
                wait(pe, s_gate, lin(o, 1, 1))
                for k in range(CT):
                    for h in range(H2):
                        last = mm(w_ps[1][:, P * k:P * k + P], yg[:, h, P * k:P * k + P], out_wT[:, h],
                                  start=(h == 0), stop=(h == 1))
                last.then_inc(s_o, 1)

            def window(g, q, last, post, prep):
                for n in range(NS):
                    if n + 1 < NS:
                        bcast(g, q, n + 1)
                    elif prep is not None:
                        bcast(prep, 1 - q, 0)
                    if n >= 2:
                        summed(g, n - 2)
                    elif last is not None:
                        summed(last, NS + n - 2)
                    if n == 2 and prep is not None:
                        p_transpose(prep)
                    if n in (3, 4) and prep is not None:
                        p_conv(prep, 1 - q, n - 3)
                    if n == 5 and prep is not None:
                        p_skip(prep, 1 - q, 0)
                        p_skip(prep, 1 - q, 1)
                    if n == 6 and post is not None:
                        if prep is not None:
                            wait(pe, s_sg, lin(prep, 2, 1))
                        project(post)
                    if n == 7 and prep is not None:
                        p_dtr(prep, 1 - q)
                    if n == 8 and prep is not None:
                        p_bc(prep, 1 - q, post)
                    if n == 9 and prep is not None:
                        p_z(prep)

            ffn(0)
            pe.wait_ge(s_dc, 11)
            p_transpose(0)
            p_conv(0, 0, 0)
            p_conv(0, 0, 1)
            p_skip(0, 0, 0)
            p_skip(0, 0, 1)
            p_dtr(0, 0)
            p_bc(0, 0, None)
            p_z(0)
            bcast(0, 0, 0)
            window(0, 0, None, None, 1)
            with pe.Fori(0, (NCH - 2) // 2) as i:
                window((i, 2, 1), 1, (i, 2, 0), (i, 2, 0), (i, 2, 2))
                window((i, 2, 2), 0, (i, 2, 1), (i, 2, 1), (i, 2, 3))
            window(NCH - 1, 1, NCH - 2, NCH - 2, None)
            summed(NCH - 1, NS - 2)
            summed(NCH - 1, NS - 1)
            project(NCH - 1)
            ffn(1)

        @block.vector
        def _(dve):
            v = nc.vector
            chain = [0]

            def link(ins):
                chain[0] += 1
                ins.then_inc(own, 1)
                dve.wait_ge(own, chain[0])

            def bc(ap, axis, shape):
                return ap.unsqueeze(axis).broadcast_to(shape)

            v.memset(wbcT[:, :, :], 0.0).then_inc(s_dc, 1)
            v.memset(xs[:, :, :], 0.0).then_inc(s_zero, 1)

            def consts():
                dve.wait_ge(s_pc, 9)
                link(v.tensor_reduce(rowsel[:, :], ident[:, :].rearrange("p (j n) -> p n j", j=4), AX, ALU.add))
                for k in range(4):
                    v.tensor_copy(sel[:, 8 * k:8 * k + 8, :],
                                  bc(rowsel[:, 8 * k:8 * k + 8], 2, [P, 8, P])).then_inc(s_dc, 1)
                dve.wait_ge(s_par, 16 * 10)
                dve.wait_ge(s_ea, 1)
                v.tensor_scalar(negA[:, :], expA[:, :], -1.0, None, ALU.mult).then_inc(s_dc, 1)
                link(v.tensor_scalar(in_wT[:, :], in_wT[:, :], norm_w, None, ALU.mult))
                v.tensor_scalar(skip_wT[:, :], skip_wT[:, :], norm_w, None, ALU.mult).then_inc(s_dc, 1)
                for k in range(TAPS):
                    v.tensor_tensor(cw[:, k], cw[:, k], in_wT[:, :], ALU.mult).then_inc(s_dc, 1)

            def moments(st, m):
                half = D // 2
                v.tensor_tensor(m[:, 0], st[:, :, 1], st[:, :, 4], ALU.add)
                v.tensor_tensor(m[:, 1], st[:, :, 1], st[:, :, 4], ALU.subtract)
                yield v.tensor_tensor(m[:, 2], st[:, :, 2], st[:, :, 5], ALU.add)
                v.tensor_scalar(m[:, 0], m[:, 0], 0.5, None, ALU.mult)
                v.tensor_scalar(m[:, 2], m[:, 2], 0.5 / half, None, ALU.mult)
                yield v.scalar_tensor_tensor(out=m[:, 1], in0=m[:, 1], scalar=0.25, in1=m[:, 1],
                                             op0=ALU.mult, op1=ALU.mult)
                yield v.tensor_tensor(m[:, 3], m[:, 1], m[:, 2], ALU.add)

            def ffn(f):
                for t in range(NT):
                    if f == 0 and t % 4 == 0:
                        dve.wait_ge(s_x[t // 4], 16)
                    last = v.bn_stats(stat[:, t, :], X[:, t, :])
                link(last)
                for part in moments(stat, mom):
                    link(part)
                mean, var = mom[:, 0], mom[:, 3]
                link(v.tensor_scalar(lnin[:, 0], var, EPS, None, ALU.add))
                link(v.reciprocal(inv[:, :], lnin[:, 0]))
                link(v.tensor_tensor(lnin[:, 1], var, inv[:, :], ALU.mult))
                v.tensor_scalar(lnin[:, 1], lnin[:, 1], EPS, None, ALU.add).then_inc(s_lnin, 1)
                dve.wait_ge(s_rst, f + 1)
                link(v.tensor_tensor(r12[:, :], rst[:, 0], rst[:, 1], ALU.mult))
                for t in range(NT):
                    v.tensor_scalar(xh[:, t, :], X[:, t, :], mean[:, t:t + 1], r12[:, t:t + 1],
                                    ALU.subtract, ALU.mult).then_inc(s_xh, 1)
                link(v.tensor_scalar(xa[:, :], rst[:, 0], 0.5, None, ALU.mult))
                link(v.tensor_tensor(xb[:, :], xa[:, :], mean, ALU.mult))
                link(v.tensor_scalar(xa[:, :], xa[:, :], 1.0, None, ALU.add))
                dve.wait_ge(s_sc, NT // 4 * (f + 1))
                link(v.tensor_copy(score[:, :, :], sc_ps))
                link(v.tensor_reduce(mx[:, :], score[:, :, :], AX, ALU.max))
                cand = tmpA[:, :].rearrange("p (t e) -> p t e", e=E)
                link(v.tensor_tensor(cand, score[:, :, :], bc(mx[:, :], 2, [P, NT, E]), ALU.is_equal))
                link(v.tensor_tensor(cand, cand, bc(desc[:, :], 1, [P, NT, E]), ALU.mult))
                link(v.tensor_reduce(best[:, :], cand, AX, ALU.max))
                v.tensor_tensor(oh[:, :, :].rearrange("p e t -> p t e"), cand, bc(best[:, :], 2, [P, NT, E]),
                                ALU.is_equal).then_inc(s_oh, 1)
                link(v.tensor_tensor(zal[:, :], mx[:, :], lnin[:, 1], ALU.mult))
                v.tensor_tensor(zal[:, :], zal[:, :], rst[:, 1], ALU.mult).then_inc(s_z, 1)
                dve.wait_ge(s_rank, f + 1)
                link(v.tensor_copy(tot[:, :], tot_ps))
                link(v.tensor_tensor_scan(out=tmpA[:, :], data0=ones_f[:, :], data1=tot[:, :], initial=0.0,
                                          op0=ALU.mult, op1=ALU.add))
                ends = tmpA[:, :].rearrange("p (e t) -> p e t", t=NT)[:, :, NT - 1]
                link(v.tensor_reduce(small[:, 0], tot[:, :].rearrange("p (e t) -> p e t", t=NT), AX, ALU.add))
                link(v.tensor_tensor(small[:, 1], ends, small[:, 0], ALU.subtract))
                link(v.tensor_tensor(tmpB[:, :], tmpA[:, :], tot[:, :], ALU.subtract))
                link(v.tensor_scalar(nti[:, 0], small[:, 0], float(P - 1), None, ALU.add))
                link(v.tensor_scalar(nti[:, 1], nti[:, 0], P.bit_length() - 1, None, ALU.logical_shift_right))
                link(v.tensor_copy(small[:, 2], nti[:, 1]))
                link(v.tensor_tensor_scan(out=small[:, 3], data0=ones_f[:, 0:E], data1=small[:, 2], initial=0.0,
                                          op0=ALU.mult, op1=ALU.add))
                link(v.tensor_tensor(small[:, 4], small[:, 3], small[:, 2], ALU.subtract))
                link(v.scalar_tensor_tensor(out=small[:, 5], in0=small[:, 4], scalar=float(P), in1=small[:, 1],
                                            op0=ALU.mult, op1=ALU.subtract))
                link(v.tensor_tensor(tmpB[:, :], tmpB[:, :], rank_ps, ALU.add))
                pos = tmpB[:, :].rearrange("p (e t) -> p e t", t=NT)
                link(v.tensor_tensor(pos, pos, bc(small[:, 5], 2, [P, E, NT]), ALU.add))
                link(v.tensor_tensor(pos, pos, oh[:, :, :], ALU.mult))
                link(v.tensor_reduce(slot_f[:, :], pos.rearrange("p e t -> p t e"), AX, ALU.add))
                v.tensor_copy(slot[:, :], slot_f[:, :]).then_inc(s_slot, 1)
                link(v.tensor_tensor(cmp[:, :, :], bc(small[:, 3], 1, [P, ST, E]), bc(jcon[:, :], 2, [P, ST, E]),
                                     ALU.is_le))
                link(v.tensor_reduce(texf[:, :], cmp[:, :, :], AX, ALU.add))
                link(v.tensor_scalar(tex[:, :], texf[:, :], float(E - 1), None, ALU.min))
                dve.wait_ge(s_ez, f + 1)
                link(v.tensor_scalar(eal[:, :], eal[:, :], 1.0, None, ALU.add))
                link(v.reciprocal(eal[:, :], eal[:, :]))
                link(v.tensor_scalar(half_alpha[:, :], eal[:, :], 0.5, None, ALU.mult))
                for t in range(NT):
                    last = v.tensor_scalar(X[:, t, :], X[:, t, :], xa[:, t:t + 1], xb[:, t:t + 1],
                                           ALU.mult, ALU.subtract)
                link(last)
                if f == 0:
                    consts()
                    dve.wait_ge(s_w, 32)

                def fetch(j, s):
                    e = dve.value_load(tex[0:1, at(j, 1)], min_val=0, max_val=E - 1)
                    wait(dve, s_y, lin(j, 1, ST * f - 2))
                    wait(dve, s_ys, lin(j, 1, ST * f - 2))
                    v.tensor_copy(wcur[:, s, :], wall[:, bass.ds(e, 1), :].rearrange("p o w -> p (o w)")
                                  ).then_inc(s_wc, 1)

                def relu(j, s):
                    wait(dve, s_h, lin(j, 1, ST * f + 1))
                    wait(dve, s_y, lin(j, 1, ST * f - 2))
                    for c in (2, 3):
                        v.tensor_scalar(hT[:, s, c], hd_ps[j % 2][:, P * (c - 2):P * (c - 2) + P],
                                        wcur[:, s, O_B1 + c:O_B1 + c + 1], 0.0,
                                        ALU.add, ALU.max).then_inc(s_rd, 1)

                def result(j, s, g):
                    wait(dve, s_y, lin(j, 1, ST * f + 1))
                    if s == 0 and g >= YR:
                        dve.wait_ge(s_yst, 16 * (NG * f + g - YR + 1))
                    v.tensor_tensor(ys[:, GT * (g % YR) + s, :], y_ps[j % 2],
                                    wcur[:, s, O_B2:PK], ALU.add).then_inc(s_ys, 1)

                fetch(0, 0)
                fetch(1, 1)
                for g in range(NG):
                    for s in range(GT):
                        j = GT * g + s
                        relu(j, s)
                        if j >= 1:
                            result(j - 1, (s - 1) % GT, (j - 1) // GT)
                        if j + 2 < ST:
                            fetch(j + 2, (s + 2) % GT)
                result(ST - 1, GT - 1, NG - 1)
                for t in range(NT):
                    r = t % (XR * GT)
                    uses = -(-NT // (XR * GT)) if r < NT % (XR * GT) or NT % (XR * GT) == 0 else NT // (XR * GT)
                    dve.wait_ge(s_g[r], 16 * (uses * f + t // (XR * GT) + 1))
                    v.scalar_tensor_tensor(out=X[:, t, :], in0=gath[:, r, :], scalar=half_alpha[:, t:t + 1],
                                           in1=X[:, t, :], op0=ALU.mult, op1=ALU.add).then_inc(s_x1, 1)

            KN = 11
            own2 = s_own2

            def prep_stats(p):
                if isinstance(p, int) and p == 0:
                    dve.wait_ge(s_x1, CT)
                elif isinstance(p, int) and p == 1:
                    dve.wait_ge(s_x1, NT)
                for k in range(CT):
                    last = v.bn_stats(cst[:, k, :], X[:, at(p, CT, k, 1), :].rearrange("p o d -> p (o d)"))
                step(last, p, 1)
                for k, part in enumerate(moments(cst, cmom)):
                    step(part, p, 2 + k)
                step(v.tensor_scalar(csm[:, 0], cmom[:, 3], EPS, None, ALU.add), p, 5)
                step(v.reciprocal(csm[:, 6], csm[:, 0]), p, 6)
                step(v.tensor_tensor(csm[:, 7], cmom[:, 3], csm[:, 6], ALU.mult), p, 7)
                v.tensor_scalar(csm[:, 1], csm[:, 7], EPS, None, ALU.add).then_inc(s_cln, 1)

            def step(ins, p, k):
                ins.then_inc(own2, 1)
                wait(dve, own2, lin(p, KN, k))

            def prep_norm(p):
                wait(dve, s_cr, lin(p, 1, 1))
                step(v.tensor_tensor(csm[:, 7], csm[:, 4], csm[:, 5], ALU.mult), p, 8)
                step(v.tensor_tensor(csm[:, 8], csm[:, 4], cmom[:, 0], ALU.mult), p, 9)
                step(v.tensor_scalar(csm[:, 9], csm[:, 4], 1.0, None, ALU.add), p, 10)
                wait(dve, s_u0, lin(p, 1, 0))
                for k in range(CT):
                    ins = v.tensor_scalar(xr[:, k, :], X[:, at(p, CT, k, 1), :].rearrange("p o d -> p (o d)"),
                                          cmom[:, 0, k:k + 1], csm[:, 7, k:k + 1], ALU.subtract, ALU.mult)
                ins.then_inc(s_xr, 1)
                for k in range(CT):
                    xk = X[:, at(p, CT, k, 1), :].rearrange("p o d -> p (o d)")
                    ins = v.tensor_scalar(xk, xk, csm[:, 9, k:k + 1], csm[:, 8, k:k + 1], ALU.mult, ALU.subtract)
                step(ins, p, 11)

            def prep_split(p, q):
                wait(dve, s_hi, lin(p, 1, 1))
                step3(v.tensor_tensor(bcr[64:128, :], w_ps[1][64:128, :], bcs[64:128, q], ALU.subtract), p, 1)
                step3(v.tensor_copy(bcs[64:128, q], bcr[64:128, :]), p, 2)
                step3(v.tensor_tensor(bcr[96:128, :], bcr[96:128, :], bcs[96:128, q], ALU.subtract), p, 3)
                v.tensor_copy(bcs[96:128, q], bcr[96:128, :]).then_inc(s_split, 1)

            def step3(ins, p, k):
                ins.then_inc(s_own3, 1)
                wait(dve, s_own3, lin(p, 3, k))

            def prep_dt(p, q):
                for h in range(H2):
                    wait(dve, s_zz, lin(p, 2, h + 1))
                    wait(dve, s_abs, lin(p, 2, h + 1))
                    v.tensor_scalar(dt[:, q, h], w_ps[h][:, :], wd2_b[:, h:h + 1], 0.0,
                                    ALU.add, ALU.max).then_inc(s_rz, 1)
                for h in range(H2):
                    wait(dve, s_sp, lin(p, 2, h + 1))
                    wait(dve, s_rz, lin(p, 2, h + 1))
                    v.tensor_tensor(dt[:, q, h], dt[:, q, h], sp_t[:, h], ALU.add).then_inc(s_dt, 1)

            def dtxb(g, q, n):
                if n == 0:
                    wait(dve, s_u, lin(g, 1, 1))
                wait(dve, s_b, lin(g, NS, n + 1))
                wait(dve, s_scan, lin(g, 2 * NS, 2 * (n - 2) + 2))
                v.tensor_tensor(bu[:, n % 2], u[:, q], bc(b_ps[n % 2][:, :], 1, [P, H2, C]),
                                ALU.mult).then_inc(s_bu, 1)

            def save_carry(g, n):
                wait(dve, s_scan, lin(g, 2 * NS, 2 * n + 2))
                v.tensor_copy(carry[:, n, :], hb[:, n % 2, :, C - 1]).then_inc(s_car, 1)

            def scan(g, q, n):
                wait(dve, s_dA, lin(g, 2 * NS, 2 * n + 2))
                wait(dve, s_bu, lin(g, NS, n + 1))
                wait(dve, s_hc, lin(g, NS, n - 1))
                if q == 1:
                    if n == 0:
                        wait(dve, s_car, lin(g, NS // 2, NS // 2))
                for h in range(H2):
                    v.tensor_tensor_scan(out=hb[:, n % 2, h], data0=dA[:, n % 4, h], data1=bu[:, n % 2, h],
                                         initial=0.0 if q == 0 else carry[:, n, h:h + 1],
                                         op0=ALU.mult, op1=ALU.add).then_inc(s_scan, 1)

            def post_read(o, q):
                wait(dve, s_gate, lin(o, 1, 0))
                wait(dve, s_o, lin(o, 1, 0))
                wait(dve, s_acc, lin(o, 2 * NS, 2 * NS))
                for h in range(H2):
                    v.scalar_tensor_tensor(out=yg[:, h], in0=xc[:, q, h], scalar=w_D[:, h:h + 1],
                                           in1=acc_ps[h][:, :], op0=ALU.mult, op1=ALU.add).then_inc(s_yg, 1)

            def post_add(o):
                wait(dve, s_o, lin(o, 1, 1))
                xk = X[:, at(o, CT), :]
                v.tensor_tensor(xk, xk, w_ps[1][:, :].rearrange("p (t d) -> p t d", d=D), ALU.add).then_inc(s_x2, 1)

            def window(g, q, nxt, post, prep):
                for n in range(NS):
                    if q == 0 and n >= 1:
                        save_carry(g, n - 1)
                    if n == 2 and post is not None:
                        post_read(post, 1 - q)
                    if n + 1 < NS:
                        dtxb(g, q, n + 1)
                    elif nxt is not None:
                        dtxb(nxt, 1 - q, 0)
                    scan(g, q, n)
                    if prep is not None:
                        if n == 0:
                            prep_stats(prep)
                        if n == 1:
                            prep_norm(prep)
                        if n == 9:
                            prep_split(prep, 1 - q)
                        if n == 11:
                            prep_dt(prep, 1 - q)
                    if n == 8 and post is not None:
                        post_add(post)
                if q == 0:
                    save_carry(g, NS - 1)

            ffn(0)
            prep_stats(0)
            prep_norm(0)
            prep_split(0, 0)
            prep_dt(0, 0)
            dtxb(0, 0, 0)
            window(0, 0, 1, None, 1)
            with dve.Fori(0, (NCH - 2) // 2) as i:
                window((i, 2, 1), 1, (i, 2, 2), (i, 2, 0), (i, 2, 2))
                window((i, 2, 2), 0, (i, 2, 3), (i, 2, 1), (i, 2, 3))
            window(NCH - 1, 1, None, NCH - 2, None)
            post_read(NCH - 1, 1)
            post_add(NCH - 1)
            dve.wait_ge(s_x2, NCH)
            ffn(1)


def kernel(**inputs):
    import numpy as np
    import concourse.bacc as bacc
    from concourse.bass_utils import run_bass_kernel_spmd as run

    i = {k: np.asarray(x) for k, x in inputs.items()}
    m = {k[len("L0_attn_"):]: x for k, x in i.items() if k.startswith("L0_attn_")}
    f = {k[len("L0_ffn_"):]: x for k, x in i.items() if k.startswith("L0_ffn_")}

    def halves(w):
        return w.reshape(2, 128, -1).transpose(1, 0, 2)

    arrays = {
        "x": m["resid"].reshape(4096, 128),
        "centT": f["centroids"].T,
        "experts": np.concatenate([
            f["W1"].transpose(2, 0, 1),
            f["W2"].reshape(8, 128, 4, 128).transpose(3, 0, 2, 1).reshape(128, 8, 512),
            f["b1"].reshape(8, 4, 128).transpose(2, 0, 1),
            f["gamma"].T[:, :, None], f["beta"].T[:, :, None]], axis=2),
        "b2": f["b2"],
        "par": np.concatenate([
            halves(m["A_log"]).reshape(128, 32),
            m["conv_b"].reshape(2, 128).T, m["wd2_b"].reshape(2, 128).T, m["W_D"].reshape(2, 128).T,
            m["norm_w"][:, None]], axis=1),
        "in_wT": m["in_w"].T,
        "skip_wT": m["skip_w"].T,
        "conv_wT": m["conv_w"].T,
        "wd1T": halves(m["wd1"].T),
        "wd2T": m["wd2"].T,
        "wbcT": halves(np.concatenate([m["wb"], m["wc"]], axis=0).T),
        "out_wT": halves(m["out_w"].T),
    }
    arrays = {k: np.ascontiguousarray(x) for k, x in arrays.items()}
    nc = bacc.Bacc("TRN2", target_bir_lowering=False, num_devices=1)
    aps = {k: nc.dram_tensor("in_" + k, x.shape, mybir.dt.float32, kind="ExternalInput").ap() for k, x in arrays.items()}
    out = nc.dram_tensor("out_y", (4096, 128), mybir.dt.float32, kind="ExternalOutput").ap()
    build(nc, aps, out)
    r = run(nc, [{"in_" + k: x for k, x in arrays.items()}], core_ids=[0])
    return r.results[0]["out_y"].reshape(4, 1024, 128)
```

```python
from contextlib import ExitStack

import concourse.bass as bass
from concourse import mybir

ALU = mybir.AluOpType
ACT = mybir.ActivationFunctionType
F32 = mybir.dt.float32
BF16 = mybir.dt.bfloat16
I32 = mybir.dt.int32
AX = mybir.AxisListType.X

P = 128
D = 128
E = 8
F = 512
FC = F // P
TOK = 4096
NT = TOK // P
ST = NT + E - 1
GT = 3
NG = ST // GT
XR = 4
YR = 4
PK = F + FC * D + FC + 2 + D
O_W2, O_B1 = F, F + FC * D
O_G, O_B, O_B2 = O_B1 + FC, O_B1 + FC + 1, O_B1 + FC + 2
EPS = 1e-5

H2 = 2
NS = 16
R = 64
TAPS = 4
C = 512
CT = C // P
NCH = TOK // C
HIST = 4
LOOPS = (NCH - 4) // 2
assert ST % GT == 0 and NT % 4 == 0


def lin(i, k, c):
    if isinstance(i, tuple):
        reg, a, b = i
        return reg * (a * k) + (b * k + c)
    return k * i + c


def wait(eng, sem, value):
    if not isinstance(value, int) or value > 0:
        eng.wait_ge(sem, value)


def at(i, size, off=0, n=None):
    n = size if n is None else n
    v = lin(i, size, off)
    return slice(v, v + n) if isinstance(v, int) else bass.ds(v, n)


def build(nc, a, out):
    with ExitStack() as ctx:
        def sb(name, shape, dt=F32):
            return ctx.enter_context(nc.sbuf_tensor(name, shape, dt))

        def ps(name, shape):
            return ctx.enter_context(nc.psum_tensor(name, shape, F32))

        def sem(name):
            return ctx.enter_context(nc.semaphore(name))

        X = sb("X", [P, NT, D])
        wall = sb("wall", [P, E, PK])
        centT = sb("centT", [D, E])
        DA, HB, HC = 4 * H2 * C, 4 * H2 * C, 4 * H2 * C
        XHN, WCN, YSN, XSN = NT * D, 3 * PK, YR * GT * D, XR * GT * D
        region = sb("region", [P, max(DA + HB + HC, XHN + WCN + YSN + XSN)])
        xh = region[:, 0:XHN].rearrange("p (t d) -> p t d", d=D)
        wcur = region[:, XHN:XHN + WCN].rearrange("p (r w) -> p r w", w=PK)
        ys = region[:, XHN + WCN:XHN + WCN + YSN].rearrange("p (t d) -> p t d", d=D)
        dA = region[:, 0:DA].rearrange("p (r h c) -> p r h c", r=4, h=H2)
        hb = region[:, DA:DA + HB].rearrange("p (r h c) -> p r h c", r=4, h=H2)
        hc = region[:, DA + HB:DA + HB + HC].rearrange("p (r h c) -> p r h c", r=4, h=H2)
        o = XHN + WCN + YSN
        xs = region[:, o:o + XSN].rearrange("p (t d) -> p t d", d=D)
        gath = xs
        xsT = sb("xsT", [D, 3, P])
        stat = sb("stat", [P, NT, 6])
        mom = sb("mom", [P, 4, NT])
        lnin = sb("lnin", [P, 2, NT])
        lnl = sb("lnl", [P, 2, NT])
        rst = sb("rst", [P, 2, NT])
        inv = sb("inv", [P, NT])
        r12 = sb("r12", [P, NT])
        xa = sb("xa", [P, NT])
        xb = sb("xb", [P, NT])
        score = sb("score", [P, NT, E])
        tmpA = sb("tmpA", [P, NT * E])
        tmpB = sb("tmpB", [P, NT * E])
        tot = sb("tot", [P, NT * E])
        oh = sb("oh", [P, E, NT], BF16)
        mx = sb("mx", [P, NT])
        best = sb("best", [P, NT])
        zal = sb("zal", [P, NT])
        eal = sb("eal", [P, NT])
        half_alpha = sb("half_alpha", [P, NT])
        slot_f = sb("slot_f", [P, NT])
        slot = sb("slot", [P, NT], I32)
        small = sb("small", [P, 8, E])
        nti = sb("nti", [P, 2, E], I32)
        cmp = sb("cmp", [P, ST, E])
        texf = sb("texf", [P, ST])
        tex = sb("tex", [P, ST], I32)
        ident = sb("ident", [P, P])
        upper = sb("upper", [P, P], BF16)
        ones_b = sb("ones_b", [P, P], BF16)
        ones_f = sb("ones_f", [P, NT * E])
        desc = sb("desc", [P, E])
        jcon = sb("jcon", [P, ST])
        rowsel = sb("rowsel", [P, 32])
        sel = sb("sel", [P, 32, P], BF16)
        par = sb("par", [P, 2 * NS + 7])
        alog = par[:, 0:2 * NS]
        conv_b = par[:, 2 * NS:2 * NS + 2]
        wd2_b = par[:, 2 * NS + 2:2 * NS + 4]
        w_D = par[:, 2 * NS + 4:2 * NS + 6]
        norm_w = par[:, 2 * NS + 6:2 * NS + 7]
        expA = sb("expA", [P, 2 * NS])
        negA = sb("negA", [P, 2 * NS])
        in_wT = sb("in_wT", [D, H2 * P])
        skip_wT = sb("skip_wT", [D, H2 * P])
        cw = sb("cw", [P, TAPS, H2 * P])
        wd2T = sb("wd2T", [R, H2 * P])
        wrbcT = sb("wrbcT", [P, H2, P])
        out_wT = sb("out_wT", [P, H2, D])
        xr = sb("xr", [P, CT, D])
        xrT = sb("xrT", [D, 2, HIST + C])
        cst = sb("cst", [P, CT, 6])
        cmom = sb("cmom", [P, 4, CT])
        csm = sb("csm", [P, 11, CT])
        xc = sb("xc", [P, 2, H2, C])
        sg = sb("sg", [P, 2, H2, C])
        dt = sb("dt", [P, 2, H2, C])
        u = sb("u", [P, 2, H2, C])
        dtr = sb("dtr", [R, C])
        bcs = sb("bcs", [P, 2, C], BF16)
        bcr = sb("bcr", [P, C])
        sp_t = sb("sp_t", [P, H2, C])
        bu = sb("bu", [P, 2, H2, C])
        cs = sb("cs", [P, 4, C])
        yg = sb("yg", [P, H2, C])
        ftT = yg
        hT = bu[:, :, :, :].rearrange("p r h c -> p (r h c)")[:, 0:3 * FC * P].rearrange(
            "p (r c t) -> p r c t", r=3, c=FC)
        carry = sb("carry", [P, NS, H2])

        bank = [ps(f"bank{i}", [P, 512]) for i in range(8)]
        tr_ps = [bank[0], bank[1]]
        sc_ps = bank[2][:, 0:NT * E].rearrange("p (t e) -> p t e", e=E)
        rank_ps, tot_ps = bank[3][:, 0:NT * E], bank[3][:, NT * E:2 * NT * E]
        xt_ps = [bank[4][:, 0:P], bank[3][:, 0:P]]
        ha_ps = [bank[5], bank[7]]
        hd_ps = [bank[6], bank[2]]
        y_ps = [bank[0][:, 0:D], bank[1][:, 0:D]]
        w_ps = [bank[0], bank[1]]
        b_ps = [bank[2], bank[3]]
        c_ps = [bank[4], bank[5]]
        acc_ps = [bank[6], bank[7]]

        rows_d = nc.dram_tensor("sorted_rows", [ST * P, D], F32, kind="Internal").ap()
        res_d = nc.dram_tensor("sorted_results", [ST * P, D], F32, kind="Internal").ap()
        rows_v = rows_d.rearrange("(t p) d -> p t d", p=P)
        res_v = res_d.rearrange("(t p) d -> p t d", p=P)
        x_v = a["x"].rearrange("(t p) d -> p t d", p=P)
        out_v = out.rearrange("(t p) d -> p t d", p=P)

        s_x = [sem(f"x_loaded{i}") for i in range(NT // 4)]
        s_par = sem("params_loaded")
        s_w = sem("expert_weights_loaded")
        s_cent = sem("centroids_loaded")
        s_zero = sem("xs_zeroed")
        s_zst = sem("rows_zeroed")
        s_pc = sem("pool_consts")
        s_dc = sem("dve_consts")
        s_ea = sem("exp_a_log")
        own = sem("dve_chain")
        s_lnin = sem("variances_ready")
        s_lnl = sem("logs_ready")
        s_rst = sem("rstd_ready")
        s_xh = sem("normed_ready")
        s_trA = sem("normed_transposed")
        s_ftT = sem("normedT_copied")
        s_sc = sem("scores_done")
        s_z = sem("alpha_arg_ready")
        s_ez = sem("alpha_exp_done")
        s_oh = sem("onehot_ready")
        s_rank = sem("ranks_done")
        s_slot = sem("slots_ready")
        s_tex = sem("tile_experts_ready")
        s_scat = sem("rows_scattered")
        s_xs = [sem(f"sorted_loaded{i}") for i in range(NG)]
        s_xt = sem("sorted_transposed")
        s_xsT = sem("sortedT_copied")
        s_wc = sem("weights_current")
        s_h = sem("hidden_done")
        s_ra = sem("relu_act_done")
        s_rd = sem("relu_dve_done")
        s_y = sem("result_done")
        s_ys = sem("result_copied")
        s_yst = sem("results_stored")
        s_g = [sem(f"gathered{i}") for i in range(XR * GT)]
        s_x1 = sem("ffn_residual_added")
        s_out = sem("output_stored")
        s_cln = sem("m_variances_ready")
        s_cl = sem("m_logs_ready")
        s_cr = sem("m_rstd_ready")
        s_nb = sem("m_scale_bias_ready")
        s_xr = sem("m_normed_ready")
        s_u0 = sem("m_transposed")
        s_xrT = sem("m_normedT_copied")
        s_hist = sem("m_history_copied")
        s_conv = sem("m_conv_done")
        s_skip = sem("m_skip_done")
        s_xc = sem("m_x_ready")
        s_sg = sem("m_gate_ready")
        s_rbc = sem("m_dtrank_bc_done")
        s_dtc = sem("m_dtrank_copied")
        s_hi = sem("m_bc_high_part")
        s_split = sem("m_bc_split")
        s_zz = sem("m_dtarg_done")
        s_abs = sem("m_dtarg_abs")
        s_ex = sem("m_softplus_exp")
        s_sp = sem("m_softplus_log")
        s_rz = sem("m_dtarg_relu")
        s_dt = sem("m_dt_ready")
        s_u = sem("m_dtx_ready")
        s_b = sem("m_b_broadcast")
        s_c = sem("m_c_broadcast")
        s_cs = sem("m_c_copied")
        s_dA = sem("m_decay_ready")
        s_bu = sem("m_dtxb_ready")
        s_scan = sem("m_scanned")
        s_car = sem("m_carry_saved")
        s_hc = sem("m_hc_ready")
        s_acc = sem("m_summed")
        s_yg = sem("m_y_read")
        s_gate = sem("m_gated")
        s_o = sem("m_projected")
        s_x2 = sem("m_residual_added")
        s_own2 = sem("m_norm_chain")
        s_own3 = sem("m_split_chain")

        block = ctx.enter_context(nc.Block())

        @block.sync
        def _(sp):
            for g in range(NT // 4):
                sp.dma_start(X[:, 4 * g:4 * g + 4, :], x_v[:, 4 * g:4 * g + 4, :]).then_inc(s_x[g], 16)
            sp.dma_start(centT[:, :], a["centT"]).then_inc(s_cent, 16)
            sp.dma_start(wall[:, :, 0:O_B2], a["experts"]).then_inc(s_w, 16)
            sp.dma_start(wall[:, :, O_B2:PK], a["b2"].partition_broadcast(P)).then_inc(s_w, 16)
            sp.wait_ge(s_zero, 1)
            for t in range(0, ST, XR * GT):
                n = min(XR * GT, ST - t)
                sp.dma_start(rows_v[:, t:t + n, :], xs[:, 0:n, :]).then_inc(s_zst, 16)
            for dst, src in ((par, "par"), (in_wT, "in_wT"), (skip_wT, "skip_wT"), (wd2T, "wd2T")):
                sp.dma_start(dst[:, :], a[src]).then_inc(s_par, 16)
            for dst, src in ((wrbcT, "wrbcT"), (out_wT, "out_wT")):
                sp.dma_start(dst[:, :, :], a[src]).then_inc(s_par, 16)
            sp.dma_start(cw[:, :, :], a["conv_wT"].partition_broadcast(P)).then_inc(s_par, 16)

            for f in range(2):
                sp.wait_ge(s_scat, 16 * NT * (f + 1))

                def load(g):
                    if g >= XR:
                        sp.wait_ge(s_xt, ST * f + GT * (g - XR + 1))
                    r = g % XR
                    sp.dma_start(xs[:, GT * r:GT * r + GT, :],
                                 rows_v[:, GT * g:GT * g + GT, :]).then_inc(s_xs[g], 16)

                for g in range(XR):
                    load(g)
                for g in range(NG):
                    sp.wait_ge(s_ys, ST * f + GT * (g + 1))
                    r = g % YR
                    sp.dma_start(res_v[:, GT * g:GT * g + GT, :],
                                 ys[:, GT * r:GT * r + GT, :]).then_inc(s_yst, 16)
                    if g + XR < NG:
                        load(g + XR)
            for g in range(NT // 4):
                sp.wait_ge(s_x1, NT + 4 * (g + 1))
                sp.dma_start(out_v[:, 4 * g:4 * g + 4, :], X[:, 4 * g:4 * g + 4, :]).then_inc(s_out, 16)
            sp.wait_ge(s_out, 16 * NT // 4)

        @block.gpsimd
        def _(pool):
            pool.memset(ident[:, :], 0.0).then_inc(s_pc, 1)
            pool.memset(upper[:, :], 0.0).then_inc(s_pc, 1)
            pool.memset(ones_b[:, :], 1.0).then_inc(s_pc, 1)
            pool.memset(ones_f[:, :], 1.0).then_inc(s_pc, 1)
            pool.memset(xrT[:, 0, 0:HIST], 0.0).then_inc(s_pc, 1)
            pool.wait_ge(s_pc, 5)
            pool.affine_select(out=ident[:, :], in_=ident[:, :], compare_op=ALU.not_equal, fill=1.0,
                               base=0, pattern=[[-1, P]], channel_multiplier=1).then_inc(s_pc, 1)
            pool.affine_select(out=upper[:, :], in_=upper[:, :], compare_op=ALU.is_ge, fill=1.0,
                               base=0, pattern=[[-1, P]], channel_multiplier=1).then_inc(s_pc, 1)
            pool.iota(desc[:, :], pattern=[[-1, E]], base=E, channel_multiplier=0,
                      allow_small_or_imprecise_dtypes=True).then_inc(s_pc, 1)
            pool.iota(jcon[:, :], pattern=[[1, ST]], base=0, channel_multiplier=0,
                      allow_small_or_imprecise_dtypes=True).then_inc(s_pc, 1)

            def scatter(f):
                pool.wait_ge(s_slot, f + 1)
                if f == 0:
                    pool.wait_ge(s_zst, 16 * -(-ST // (XR * GT)))
                pool.wait_ge(s_xh, NT * (f + 1))
                for t in range(NT):
                    pool.indirect_dma_start(rows_d, bass.IndirectOffsetOnAxis(ap=slot[:, t:t + 1], axis=0),
                                            xh[:, t, :], None).then_inc(s_scat, 16)

            def gather(f):
                pool.wait_ge(s_yst, 16 * NG * (f + 1))
                for t in range(NT):
                    r = t % (XR * GT)
                    if t >= XR * GT:
                        pool.wait_ge(s_x1, NT * f + t - XR * GT + 1)
                    pool.indirect_dma_start(gath[:, r, :], None, res_d,
                                            bass.IndirectOffsetOnAxis(ap=slot[:, t:t + 1], axis=0)
                                            ).then_inc(s_g[r], 16)

            def dtx(p, par_):
                wait(pool, s_dt, lin(p, 2, 2))
                wait(pool, s_xc, lin(p, 2, 2))
                pool.tensor_tensor(u[:, par_], dt[:, par_], xc[:, par_], ALU.mult).then_inc(s_u, 1)

            def gate(o, par_):
                wait(pool, s_yg, lin(o, 2, 2))
                wait(pool, s_sg, lin(o, 2, 2))
                pool.tensor_tensor(yg[:, :, :], yg[:, :, :], sg[:, par_], ALU.mult).then_inc(s_gate, 1)

            def window(g, par_, post, prep):
                for n in range(NS):
                    wait(pool, s_scan, lin(g, 2 * NS, 2 * n + 2))
                    wait(pool, s_cs, lin(g, NS, n + 1))
                    wait(pool, s_acc, lin(g, 2 * NS, 2 * (n - 4) + 2))
                    pool.tensor_tensor(hc[:, n % 4], hb[:, n % 4],
                                       cs[:, n % 4].unsqueeze(1).broadcast_to([P, H2, C]),
                                       ALU.mult).then_inc(s_hc, 1)
                    if n == 3 and post is not None:
                        gate(post, 1 - par_)
                    if n == 13 and prep is not None:
                        dtx(prep, 1 - par_)

            scatter(0)
            gather(0)
            dtx(0, 0)
            window(0, 0, None, 1)
            with pool.Fori(0, LOOPS) as i:
                window((i, 2, 1), 1, (i, 2, 0), (i, 2, 2))
                window((i, 2, 2), 0, (i, 2, 1), (i, 2, 3))
            for g in range(2 * LOOPS + 1, NCH):
                window(g, g % 2, g - 1, g + 1 if g + 1 < NCH else None)
            gate(NCH - 1, 1)
            scatter(1)
            gather(1)

        @block.scalar
        def _(act):
            nc.scalar.preload_act_table_set("natural_log_exp_and_others")

            def ffn(f):
                act.wait_ge(s_lnin, f + 1)
                nc.scalar.activation(lnl[:, :, :], lnin[:, :, :], ACT.Ln).then_inc(s_lnl, 1)
                act.wait_ge(s_lnl, f + 1)
                nc.scalar.activation(rst[:, :, :], lnl[:, :, :], ACT.Exp, scale=-0.5).then_inc(s_rst, 1)
                for g in range(NT // 4):
                    act.wait_ge(s_trA, NT // 4 * f + g + 1)
                    if g >= 2:
                        act.wait_ge(s_sc, NT // 4 * f + g - 1)
                    nc.scalar.activation(ftT[:, g % 2], tr_ps[g % 2][:, :], ACT.Copy).then_inc(s_ftT, 1)
                if f == 0:
                    act.wait_ge(s_par, 16 * 7)
                    nc.scalar.activation(expA[:, :], alog, ACT.Exp).then_inc(s_ea, 1)
                act.wait_ge(s_z, f + 1)
                nc.scalar.activation(eal[:, :], zal[:, :], ACT.Exp, scale=-1.0).then_inc(s_ez, 1)

                def tile(j, s):
                    wait(act, s_xt, lin(j, 1, ST * f + 1))
                    wait(act, s_wc, lin(j, 1, ST * f + 1))
                    wait(act, s_h, lin(j, 1, ST * f - 2))
                    nc.scalar.activation(xsT[:, s % GT], xt_ps[s % 2], ACT.Identity,
                                         scale=wcur[:, s % GT, O_G:O_G + 1],
                                         bias=wcur[:, s % GT, O_B:O_B + 1]).then_inc(s_xsT, 1)

                def relu(j, s):
                    wait(act, s_h, lin(j, 1, ST * f + 1))
                    wait(act, s_y, lin(j, 1, ST * f - 2))
                    for c in (0, 1):
                        nc.scalar.activation(hT[:, s % GT, c], ha_ps[s % 2][:, P * c:P * c + P], ACT.Relu,
                                             bias=wcur[:, s % GT, O_B1 + c:O_B1 + c + 1]).then_inc(s_ra, 1)

                U = 2 * GT

                tile(0, 0)
                for j in range(U):
                    tile(j + 1, j + 1)
                    relu(j, j)
                with act.Fori(1, ST // U) as i:
                    for s in range(U):
                        tile((i, U, s + 1), s + 1)
                        relu((i, U, s), s)
                for j in range(ST // U * U, ST):
                    if j + 1 < ST:
                        tile(j + 1, j + 1)
                    relu(j, j)

            def prep_norm(p):
                wait(act, s_cln, lin(p, 1, 1))
                nc.scalar.activation(csm[:, 2:4, :], csm[:, 0:2, :], ACT.Ln).then_inc(s_cl, 1)
                wait(act, s_cl, lin(p, 1, 1))
                nc.scalar.activation(csm[:, 4:6, :], csm[:, 2:4, :], ACT.Exp, scale=-0.5).then_inc(s_cr, 1)

            def prep_xr(p):
                wait(act, s_nb, lin(p, 1, 1))
                wait(act, s_u0, lin(p, 1, 0))
                for k in range(CT):
                    ins = nc.scalar.activation(xr[:, k, :], X[:, at(p, CT, k, 1), :].rearrange("p o d -> p (o d)"),
                                               ACT.Identity, scale=csm[:, 7, k:k + 1], bias=csm[:, 10, k:k + 1])
                ins.then_inc(s_xr, 1)

            def prep_xrT(p, q):
                wait(act, s_u0, lin(p, 1, 1))
                nc.scalar.activation(xrT[:, q, HIST:HIST + C], w_ps[0][:, :], ACT.Copy).then_inc(s_xrT, 1)
                if q == 1:
                    nc.scalar.activation(xrT[:, 1, 0:HIST], xrT[:, 0, C:C + HIST], ACT.Copy).then_inc(s_hist, 1)

            def prep_silu(p, q):
                for h in range(H2):
                    wait(act, s_conv, lin(p, 2, h + 1))
                    wait(act, s_yg, lin(p, 2, -2))
                    nc.scalar.activation(xc[:, q, h], w_ps[1 - h][:, :], ACT.Silu,
                                         bias=conv_b[:, h:h + 1]).then_inc(s_xc, 1)
                for h in range(H2):
                    wait(act, s_skip, lin(p, 2, h + 1))
                    wait(act, s_gate, lin(p, 1, -1))
                    nc.scalar.activation(sg[:, q, h], w_ps[1 - h][:, :], ACT.Silu).then_inc(s_sg, 1)
                nc.scalar.preload_act_table_set("natural_log_exp_and_others")

            def prep_rbc(p, q):
                wait(act, s_rbc, lin(p, 1, 1))
                wait(act, s_zz, lin(p, 2, 0))
                nc.scalar.activation(bcs[64:128, q], w_ps[0][64:128, :], ACT.Copy).then_inc(s_hi, 1)
                nc.scalar.activation(dtr[:, :], w_ps[0][0:R, :], ACT.Copy).then_inc(s_dtc, 1)

            def prep_softplus(p):
                for h in range(H2):
                    wait(act, s_zz, lin(p, 2, h + 1))
                    wait(act, s_dt, lin(p, 2, h - 1))
                    nc.scalar.activation(sp_t[:, h], w_ps[h][:, :], ACT.Abs,
                                         bias=wd2_b[:, h:h + 1]).then_inc(s_abs, 1)
                for h in range(H2):
                    wait(act, s_abs, lin(p, 2, h + 1))
                    nc.scalar.activation(sp_t[:, h], sp_t[:, h], ACT.Exp, scale=-1.0).then_inc(s_ex, 1)
                for h in range(H2):
                    wait(act, s_ex, lin(p, 2, h + 1))
                    nc.scalar.activation(sp_t[:, h], sp_t[:, h], ACT.Ln, bias=1.0).then_inc(s_sp, 1)

            def decay(g, q, n):
                if n == 0:
                    wait(act, s_dt, lin(g, 2, 2))
                wait(act, s_scan, lin(g, 2 * NS, 2 * (n - 4) + 2))
                for h in range(H2):
                    nc.scalar.activation(dA[:, n % 4, h], dt[:, q, h], ACT.Exp,
                                         scale=negA[:, h * NS + n:h * NS + n + 1]).then_inc(s_dA, 1)

            def copy_c(g, n):
                wait(act, s_c, lin(g, NS, n + 1))
                wait(act, s_hc, lin(g, NS, n - 3))
                nc.scalar.activation(cs[:, n % 4], c_ps[n % 2][:, :], ACT.Copy).then_inc(s_cs, 1)

            def early(a, q, n):
                if n == 8:
                    prep_norm(a)
                if n == 10:
                    prep_xr(a)
                if n == 12:
                    prep_xrT(a, q)

            def late(b, q, n):
                if n == 4:
                    prep_silu(b, q)
                if n == 6:
                    prep_rbc(b, q)
                if n == 11:
                    prep_softplus(b)

            def window(g, q, a, b):
                for n in range(NS):
                    if n + 2 < NS:
                        decay(g, q, n + 2)
                    elif b is not None:
                        decay(b, 1 - q, n + 2 - NS)
                    if n + 1 < NS:
                        copy_c(g, n + 1)
                    elif b is not None:
                        copy_c(b, 0)
                    if b is not None:
                        late(b, 1 - q, n)
                    if a is not None:
                        early(a, q, n)

            ffn(0)
            act.wait_ge(s_dc, 11)
            for n in range(NS):
                early(0, 0, n)
            for n in range(NS):
                late(0, 0, n)
                early(1, 1, n)
            decay(0, 0, 0)
            decay(0, 0, 1)
            copy_c(0, 0)
            window(0, 0, 2, 1)
            with act.Fori(0, LOOPS) as i:
                window((i, 2, 1), 1, (i, 2, 3), (i, 2, 2))
                window((i, 2, 2), 0, (i, 2, 4), (i, 2, 3))
            for g in range(2 * LOOPS + 1, NCH):
                window(g, g % 2, g + 2 if g + 2 < NCH else None, g + 1 if g + 1 < NCH else None)
            ffn(1)

        @block.tensor
        def _(pe):
            mm = nc.tensor.matmul

            def ffn(f):
                pe.wait_ge(s_pc, 9)
                if f == 0:
                    pe.wait_ge(s_cent, 16)

                def scores(g):
                    pe.wait_ge(s_ftT, NT // 4 * f + g + 1)
                    for k in range(4):
                        last = mm(sc_ps[:, 4 * g + k, :], ftT[:, g % 2, P * k:P * k + P], centT[:, :],
                                  start=True, stop=True)
                    last.then_inc(s_sc, 1)

                for g in range(NT // 4):
                    pe.wait_ge(s_xh, NT * f + 4 * (g + 1))
                    if g >= 2:
                        pe.wait_ge(s_ftT, NT // 4 * f + g - 1)
                    for k in range(4):
                        last = nc.tensor.transpose(tr_ps[g % 2][:, P * k:P * k + P], xh[:, 4 * g + k, :], ident[:, :])
                    last.then_inc(s_trA, 1)
                    if g >= 1:
                        scores(g - 1)
                scores(NT // 4 - 1)
                pe.wait_ge(s_oh, f + 1)
                oh_v = oh[:, :, :].rearrange("p e t -> p (e t)")
                mm(rank_ps, upper[:, :], oh_v, start=True, stop=True)
                mm(tot_ps, ones_b[:, :], oh_v, start=True, stop=True).then_inc(s_rank, 1)

                def transpose(j):
                    if j % GT == 0:
                        pe.wait_ge(s_xs[j // GT], 16 * (f + 1))
                    wait(pe, s_xsT, ST * f + j - 1)
                    nc.tensor.transpose(xt_ps[j % 2], xs[:, j % (XR * GT), :], ident[:, :]).then_inc(s_xt, 1)

                def hidden(j):
                    pe.wait_ge(s_wc, ST * f + j + 1)
                    pe.wait_ge(s_xsT, ST * f + j + 1)
                    wait(pe, s_ra, 2 * (ST * f + j) - 2)
                    wait(pe, s_rd, 2 * (ST * f + j) - 2)
                    for c in range(FC):
                        to = (ha_ps if c < 2 else hd_ps)[j % 2]
                        last = mm(to[:, P * (c % 2):P * (c % 2) + P], wcur[:, j % GT, P * c:P * c + P],
                                  xsT[:, j % GT], start=True, stop=True)
                    last.then_inc(s_h, 1)

                def result(j):
                    pe.wait_ge(s_ra, 2 * (ST * f + j) + 2)
                    pe.wait_ge(s_rd, 2 * (ST * f + j) + 2)
                    wait(pe, s_ys, ST * f + j - 1)
                    for c in range(FC):
                        last = mm(y_ps[j % 2], hT[:, j % GT, c],
                                  wcur[:, j % GT, O_W2 + D * c:O_W2 + D * c + D],
                                  start=(c == 0), stop=(c == FC - 1))
                    last.then_inc(s_y, 1)

                transpose(0)
                for j in range(ST):
                    if j + 1 < ST:
                        transpose(j + 1)
                    hidden(j)
                    if j >= 1:
                        result(j - 1)
                result(ST - 1)

            def p_transpose(p):
                wait(pe, s_xr, lin(p, 1, 1))
                wait(pe, s_rz, lin(p, 2, -1))
                wait(pe, s_abs, lin(p, 2, -1))
                for k in range(CT):
                    last = nc.tensor.transpose(w_ps[0][:, P * k:P * k + P], xr[:, k, :], ident[:, :])
                last.then_inc(s_u0, 1)

            def p_conv(p, q, h, taps):
                if 0 in taps:
                    wait(pe, s_xrT, lin(p, 1, 1))
                    if q == 1:
                        wait(pe, s_hist, lin(p, 1, 1) // 2 if isinstance(p, int) else lin((p[0], 1, (p[2] + 1) // 2), 1, 0))
                    if h == 0:
                        wait(pe, s_rz, lin(p, 2, 0))
                        wait(pe, s_abs, lin(p, 2, 0))
                        wait(pe, s_x2, lin(p, 1, -2))
                for k in taps:
                    o = HIST - (TAPS - 1) + k
                    last = mm(w_ps[1 - h][:, :], cw[:, k, P * h:P * h + P], xrT[:, q, o:o + C],
                              start=(k == 0), stop=(k == TAPS - 1))
                if TAPS - 1 in taps:
                    last.then_inc(s_conv, 1)

            def p_skip(p, q, h):
                wait(pe, s_xc, lin(p, 2, h + 1))
                mm(w_ps[1 - h][:, :], skip_wT[:, P * h:P * h + P], xrT[:, q, HIST:HIST + C],
                   start=True, stop=True).then_inc(s_skip, 1)

            def p_rbc(p, q, h):
                if h == 0:
                    wait(pe, s_sg, lin(p, 2, 2))
                last = mm(w_ps[0][:, :], wrbcT[:, h], xc[:, q, h], start=(h == 0), stop=(h == 1))
                if h == 1:
                    last.then_inc(s_rbc, 1)

            def p_z(p, h):
                if h == 0:
                    wait(pe, s_dtc, lin(p, 1, 1))
                    wait(pe, s_split, lin(p, 1, 1))
                else:
                    wait(pe, s_x2, lin(p, 1, -1))
                mm(w_ps[h][:, :], wd2T[:, P * h:P * h + P], dtr[:, :], start=True, stop=True).then_inc(s_zz, 1)

            def bcast(g, q, n):
                if n == 0:
                    wait(pe, s_split, lin(g, 1, 1))
                wait(pe, s_bu, lin(g, NS, n - 1))
                mm(b_ps[n % 2][:, :], sel[:, n], bcs[:, q], start=True, stop=True).then_inc(s_b, 1)
                wait(pe, s_cs, lin(g, NS, n - 1))
                mm(c_ps[n % 2][:, :], sel[:, NS + n], bcs[:, q], start=True, stop=True).then_inc(s_c, 1)

            def summed(g, n):
                wait(pe, s_hc, lin(g, NS, n + 1))
                if n == 0:
                    wait(pe, s_yg, lin(g, 2, 0))
                for h in range(H2):
                    mm(acc_ps[h][:, :], ident[:, :], hc[:, n % 4, h], start=(n == 0), stop=(n == NS - 1),
                       ).then_inc(s_acc, 1)

            def project(o, tiles):
                if 0 in tiles:
                    wait(pe, s_gate, lin(o, 1, 1))
                for k in tiles:
                    for h in range(H2):
                        last = mm(w_ps[1][:, P * k:P * k + P], yg[:, h, P * k:P * k + P], out_wT[:, h],
                                  start=(h == 0), stop=(h == 1))
                if CT - 1 in tiles:
                    last.then_inc(s_o, 1)

            def early(a, q, n):
                if n == 12:
                    p_transpose(a)
                if n >= 12:
                    p_conv(a, q, 0, (n - 12,))

            def late(b, q, n):
                if n < 4:
                    p_conv(b, q, 1, (n,))
                if n == 4:
                    p_skip(b, q, 0)
                    p_skip(b, q, 1)
                if n in (5, 6):
                    p_rbc(b, q, n - 5)
                if n in (10, 11):
                    p_z(b, n - 10)

            def window(g, q, a, b, o):
                for n in range(NS):
                    if n + 1 < NS:
                        bcast(g, q, n + 1)
                    elif b is not None:
                        bcast(b, 1 - q, 0)
                    if n >= 2:
                        summed(g, n - 2)
                    elif o is not None:
                        summed(o, NS + n - 2)
                    if b is not None:
                        late(b, 1 - q, n)
                    if o is not None and n in (7, 8):
                        if b is None:
                            wait(pe, s_rz, lin(g, 2, 2))
                            wait(pe, s_abs, lin(g, 2, 2))
                        project(o, (0, 1) if n == 7 else (2, 3))
                    if a is not None:
                        early(a, q, n)

            ffn(0)
            pe.wait_ge(s_dc, 11)
            for n in range(NS):
                early(0, 0, n)
            for n in range(NS):
                late(0, 0, n)
                early(1, 1, n)
            bcast(0, 0, 0)
            window(0, 0, 2, 1, None)
            with pe.Fori(0, LOOPS) as i:
                window((i, 2, 1), 1, (i, 2, 3), (i, 2, 2), (i, 2, 0))
                window((i, 2, 2), 0, (i, 2, 4), (i, 2, 3), (i, 2, 1))
            for g in range(2 * LOOPS + 1, NCH):
                window(g, g % 2, g + 2 if g + 2 < NCH else None, g + 1 if g + 1 < NCH else None, g - 1)
            summed(NCH - 1, NS - 2)
            summed(NCH - 1, NS - 1)
            pe.wait_ge(s_x2, NCH - 1)
            project(NCH - 1, range(CT))
            ffn(1)

        @block.vector
        def _(dve):
            v = nc.vector
            chain = [0]

            def link(ins):
                chain[0] += 1
                ins.then_inc(own, 1)
                dve.wait_ge(own, chain[0])

            def bc(ap, axis, shape):
                return ap.unsqueeze(axis).broadcast_to(shape)

            v.memset(bcs[:, :, :], 0.0).then_inc(s_dc, 1)
            v.memset(xs[:, :, :], 0.0).then_inc(s_zero, 1)

            def consts():
                dve.wait_ge(s_pc, 9)
                link(v.tensor_reduce(rowsel[:, :], ident[:, :].rearrange("p (j n) -> p n j", j=4), AX, ALU.add))
                for k in range(4):
                    v.tensor_copy(sel[:, 8 * k:8 * k + 8, :],
                                  bc(rowsel[:, 8 * k:8 * k + 8], 2, [P, 8, P])).then_inc(s_dc, 1)
                dve.wait_ge(s_par, 16 * 7)
                dve.wait_ge(s_ea, 1)
                v.tensor_scalar(negA[:, :], expA[:, :], -1.0, None, ALU.mult).then_inc(s_dc, 1)
                link(v.tensor_scalar(in_wT[:, :], in_wT[:, :], norm_w, None, ALU.mult))
                v.tensor_scalar(skip_wT[:, :], skip_wT[:, :], norm_w, None, ALU.mult).then_inc(s_dc, 1)
                for k in range(TAPS):
                    v.tensor_tensor(cw[:, k], cw[:, k], in_wT[:, :], ALU.mult).then_inc(s_dc, 1)

            def moments(st, m):
                half = D // 2
                v.tensor_tensor(m[:, 0], st[:, :, 1], st[:, :, 4], ALU.add)
                v.tensor_tensor(m[:, 1], st[:, :, 1], st[:, :, 4], ALU.subtract)
                yield v.tensor_tensor(m[:, 2], st[:, :, 2], st[:, :, 5], ALU.add)
                v.tensor_scalar(m[:, 0], m[:, 0], 0.5, None, ALU.mult)
                v.tensor_scalar(m[:, 2], m[:, 2], 0.5 / half, None, ALU.mult)
                yield v.scalar_tensor_tensor(out=m[:, 1], in0=m[:, 1], scalar=0.25, in1=m[:, 1],
                                             op0=ALU.mult, op1=ALU.mult)
                yield v.tensor_tensor(m[:, 3], m[:, 1], m[:, 2], ALU.add)

            def ffn(f):
                for t in range(NT):
                    if f == 0 and t % 4 == 0:
                        dve.wait_ge(s_x[t // 4], 16)
                    last = v.bn_stats(stat[:, t, :], X[:, t, :])
                link(last)
                for part in moments(stat, mom):
                    link(part)
                mean, var = mom[:, 0], mom[:, 3]
                link(v.tensor_scalar(lnin[:, 0], var, EPS, None, ALU.add))
                link(v.reciprocal(inv[:, :], lnin[:, 0]))
                link(v.tensor_tensor(lnin[:, 1], var, inv[:, :], ALU.mult))
                v.tensor_scalar(lnin[:, 1], lnin[:, 1], EPS, None, ALU.add).then_inc(s_lnin, 1)
                dve.wait_ge(s_rst, f + 1)
                link(v.tensor_tensor(r12[:, :], rst[:, 0], rst[:, 1], ALU.mult))
                for t in range(NT):
                    v.tensor_scalar(xh[:, t, :], X[:, t, :], mean[:, t:t + 1], r12[:, t:t + 1],
                                    ALU.subtract, ALU.mult).then_inc(s_xh, 1)
                link(v.tensor_scalar(xa[:, :], rst[:, 0], 0.5, None, ALU.mult))
                link(v.tensor_tensor(xb[:, :], xa[:, :], mean, ALU.mult))
                link(v.tensor_scalar(xa[:, :], xa[:, :], 1.0, None, ALU.add))
                dve.wait_ge(s_sc, NT // 4 * (f + 1))
                link(v.tensor_copy(score[:, :, :], sc_ps))
                link(v.tensor_reduce(mx[:, :], score[:, :, :], AX, ALU.max))
                cand = tmpA[:, :].rearrange("p (t e) -> p t e", e=E)
                link(v.tensor_tensor(cand, score[:, :, :], bc(mx[:, :], 2, [P, NT, E]), ALU.is_equal))
                link(v.tensor_tensor(cand, cand, bc(desc[:, :], 1, [P, NT, E]), ALU.mult))
                link(v.tensor_reduce(best[:, :], cand, AX, ALU.max))
                v.tensor_tensor(oh[:, :, :].rearrange("p e t -> p t e"), cand, bc(best[:, :], 2, [P, NT, E]),
                                ALU.is_equal).then_inc(s_oh, 1)
                link(v.tensor_tensor(zal[:, :], mx[:, :], lnin[:, 1], ALU.mult))
                v.tensor_tensor(zal[:, :], zal[:, :], rst[:, 1], ALU.mult).then_inc(s_z, 1)
                dve.wait_ge(s_rank, f + 1)
                link(v.tensor_copy(tot[:, :], tot_ps))
                link(v.tensor_tensor_scan(out=tmpA[:, :], data0=ones_f[:, :], data1=tot[:, :], initial=0.0,
                                          op0=ALU.mult, op1=ALU.add))
                ends = tmpA[:, :].rearrange("p (e t) -> p e t", t=NT)[:, :, NT - 1]
                link(v.tensor_reduce(small[:, 0], tot[:, :].rearrange("p (e t) -> p e t", t=NT), AX, ALU.add))
                link(v.tensor_tensor(small[:, 1], ends, small[:, 0], ALU.subtract))
                link(v.tensor_tensor(tmpB[:, :], tmpA[:, :], tot[:, :], ALU.subtract))
                link(v.tensor_scalar(nti[:, 0], small[:, 0], float(P - 1), None, ALU.add))
                link(v.tensor_scalar(nti[:, 1], nti[:, 0], P.bit_length() - 1, None, ALU.logical_shift_right))
                link(v.tensor_copy(small[:, 2], nti[:, 1]))
                link(v.tensor_tensor_scan(out=small[:, 3], data0=ones_f[:, 0:E], data1=small[:, 2], initial=0.0,
                                          op0=ALU.mult, op1=ALU.add))
                link(v.tensor_tensor(small[:, 4], small[:, 3], small[:, 2], ALU.subtract))
                link(v.scalar_tensor_tensor(out=small[:, 5], in0=small[:, 4], scalar=float(P), in1=small[:, 1],
                                            op0=ALU.mult, op1=ALU.subtract))
                link(v.tensor_tensor(tmpB[:, :], tmpB[:, :], rank_ps, ALU.add))
                pos = tmpB[:, :].rearrange("p (e t) -> p e t", t=NT)
                link(v.tensor_tensor(pos, pos, bc(small[:, 5], 2, [P, E, NT]), ALU.add))
                link(v.tensor_tensor(pos, pos, oh[:, :, :], ALU.mult))
                link(v.tensor_reduce(slot_f[:, :], pos.rearrange("p e t -> p t e"), AX, ALU.add))
                v.tensor_copy(slot[:, :], slot_f[:, :]).then_inc(s_slot, 1)
                link(v.tensor_tensor(cmp[:, :, :], bc(small[:, 3], 1, [P, ST, E]), bc(jcon[:, :], 2, [P, ST, E]),
                                     ALU.is_le))
                link(v.tensor_reduce(texf[:, :], cmp[:, :, :], AX, ALU.add))
                link(v.tensor_scalar(tex[:, :], texf[:, :], float(E - 1), None, ALU.min))
                dve.wait_ge(s_ez, f + 1)
                link(v.tensor_scalar(eal[:, :], eal[:, :], 1.0, None, ALU.add))
                link(v.reciprocal(eal[:, :], eal[:, :]))
                link(v.tensor_scalar(half_alpha[:, :], eal[:, :], 0.5, None, ALU.mult))
                for t in range(NT):
                    last = v.tensor_scalar(X[:, t, :], X[:, t, :], xa[:, t:t + 1], xb[:, t:t + 1],
                                           ALU.mult, ALU.subtract)
                link(last)
                if f == 0:
                    consts()
                    dve.wait_ge(s_w, 32)

                def fetch(j, s):
                    e = dve.value_load(tex[0:1, at(j, 1)], min_val=0, max_val=E - 1)
                    wait(dve, s_y, lin(j, 1, ST * f - 2))
                    wait(dve, s_ys, lin(j, 1, ST * f - 2))
                    v.tensor_copy(wcur[:, s, :], wall[:, bass.ds(e, 1), :].rearrange("p o w -> p (o w)")
                                  ).then_inc(s_wc, 1)

                def relu(j, s):
                    wait(dve, s_h, lin(j, 1, ST * f + 1))
                    wait(dve, s_y, lin(j, 1, ST * f - 2))
                    for c in (2, 3):
                        v.tensor_scalar(hT[:, s, c], hd_ps[j % 2][:, P * (c - 2):P * (c - 2) + P],
                                        wcur[:, s, O_B1 + c:O_B1 + c + 1], 0.0,
                                        ALU.add, ALU.max).then_inc(s_rd, 1)

                def result(j, s, g):
                    wait(dve, s_y, lin(j, 1, ST * f + 1))
                    if s == 0 and g >= YR:
                        dve.wait_ge(s_yst, 16 * (NG * f + g - YR + 1))
                    v.tensor_tensor(ys[:, GT * (g % YR) + s, :], y_ps[j % 2],
                                    wcur[:, s, O_B2:PK], ALU.add).then_inc(s_ys, 1)

                fetch(0, 0)
                fetch(1, 1)
                for g in range(NG):
                    for s in range(GT):
                        j = GT * g + s
                        relu(j, s)
                        if j >= 1:
                            result(j - 1, (s - 1) % GT, (j - 1) // GT)
                        if j + 2 < ST:
                            fetch(j + 2, (s + 2) % GT)
                result(ST - 1, GT - 1, NG - 1)
                for t in range(NT):
                    r = t % (XR * GT)
                    uses = -(-NT // (XR * GT)) if r < NT % (XR * GT) or NT % (XR * GT) == 0 else NT // (XR * GT)
                    dve.wait_ge(s_g[r], 16 * (uses * f + t // (XR * GT) + 1))
                    v.scalar_tensor_tensor(out=X[:, t, :], in0=gath[:, r, :], scalar=half_alpha[:, t:t + 1],
                                           in1=X[:, t, :], op0=ALU.mult, op1=ALU.add).then_inc(s_x1, 1)

            KN = 11
            own2 = s_own2

            def early(a, q, n):
                if n == 3:
                    for k in range(CT):
                        last = v.bn_stats(cst[:, k, :], X[:, at(a, CT, k, 1), :].rearrange("p o d -> p (o d)"))
                    step(last, a, 1)
                if n == 4:
                    for k, part in enumerate(moments(cst, cmom)):
                        step(part, a, 2 + k)
                if n == 5:
                    step(v.tensor_scalar(csm[:, 0], cmom[:, 3], EPS, None, ALU.add), a, 5)
                    step(v.reciprocal(csm[:, 6], csm[:, 0]), a, 6)
                if n == 6:
                    step(v.tensor_tensor(csm[:, 7], cmom[:, 3], csm[:, 6], ALU.mult), a, 7)
                    v.tensor_scalar(csm[:, 1], csm[:, 7], EPS, None, ALU.add).then_inc(s_cln, 1)
                if n == 9:
                    wait(dve, s_cr, lin(a, 1, 1))
                    step(v.tensor_tensor(csm[:, 7], csm[:, 4], csm[:, 5], ALU.mult), a, 8)
                    step(v.tensor_tensor(csm[:, 8], csm[:, 4], cmom[:, 0], ALU.mult), a, 9)
                    step(v.tensor_scalar(csm[:, 9], csm[:, 4], 1.0, None, ALU.add), a, 10)
                    v.scalar_tensor_tensor(out=csm[:, 10], in0=csm[:, 7], scalar=-1.0, in1=cmom[:, 0],
                                           op0=ALU.mult, op1=ALU.mult).then_inc(s_nb, 1)
                if n == 13:
                    wait(dve, s_xr, lin(a, 1, 1))
                    for k in range(CT):
                        xk = X[:, at(a, CT, k, 1), :].rearrange("p o d -> p (o d)")
                        ins = v.tensor_scalar(xk, xk, csm[:, 9, k:k + 1], csm[:, 8, k:k + 1],
                                              ALU.mult, ALU.subtract)
                    step(ins, a, 11)

            def late(b, q, n):
                if n in (7, 8, 9):
                    prep_split(b, q, n - 7)
                if n in (11, 12, 13):
                    prep_dt(b, q, n - 11)

            def step(ins, p, k):
                ins.then_inc(own2, 1)
                wait(dve, own2, lin(p, KN, k))

            def prep_norm(p):
                wait(dve, s_cr, lin(p, 1, 1))
                step(v.tensor_tensor(csm[:, 7], csm[:, 4], csm[:, 5], ALU.mult), p, 8)
                step(v.tensor_tensor(csm[:, 8], csm[:, 4], cmom[:, 0], ALU.mult), p, 9)
                step(v.tensor_scalar(csm[:, 9], csm[:, 4], 1.0, None, ALU.add), p, 10)
                wait(dve, s_u0, lin(p, 1, 0))
                for k in range(CT):
                    ins = v.tensor_scalar(xr[:, k, :], X[:, at(p, CT, k, 1), :].rearrange("p o d -> p (o d)"),
                                          cmom[:, 0, k:k + 1], csm[:, 7, k:k + 1], ALU.subtract, ALU.mult)
                ins.then_inc(s_xr, 1)
                for k in range(CT):
                    xk = X[:, at(p, CT, k, 1), :].rearrange("p o d -> p (o d)")
                    ins = v.tensor_scalar(xk, xk, csm[:, 9, k:k + 1], csm[:, 8, k:k + 1], ALU.mult, ALU.subtract)
                step(ins, p, 11)

            def prep_split(p, q, k):
                mid = slice(96, 128)
                if k == 0:
                    wait(dve, s_hi, lin(p, 1, 1))
                    wait(dve, s_dtc, lin(p, 1, 1))
                    step3(v.tensor_tensor(bcr[mid, :], w_ps[0][mid, :], bcs[mid, q], ALU.subtract), p, 1)
                elif k == 1:
                    step3(v.tensor_copy(bcs[mid, q], bcr[mid, :]), p, 2)
                else:
                    v.tensor_tensor(bcs[0:32, q], bcr[mid, :], bcs[mid, q], ALU.subtract).then_inc(s_split, 1)

            def step3(ins, p, k):
                ins.then_inc(s_own3, 1)
                wait(dve, s_own3, lin(p, 2, k))

            def prep_dt(p, q, k):
                if k == 0:
                    for h in range(H2):
                        wait(dve, s_abs, lin(p, 2, h + 1))
                        v.tensor_scalar(dt[:, q, h], w_ps[h][:, :], wd2_b[:, h:h + 1], 0.0,
                                        ALU.add, ALU.max).then_inc(s_rz, 1)
                else:
                    h = k - 1
                    wait(dve, s_sp, lin(p, 2, h + 1))
                    wait(dve, s_rz, lin(p, 2, h + 1))
                    v.tensor_tensor(dt[:, q, h], dt[:, q, h], sp_t[:, h], ALU.add).then_inc(s_dt, 1)

            def dtxb(g, q, n):
                if n == 0:
                    wait(dve, s_u, lin(g, 1, 1))
                wait(dve, s_b, lin(g, NS, n + 1))
                wait(dve, s_scan, lin(g, 2 * NS, 2 * (n - 2) + 2))
                v.tensor_tensor(bu[:, n % 2], u[:, q], bc(b_ps[n % 2][:, :], 1, [P, H2, C]),
                                ALU.mult).then_inc(s_bu, 1)

            def save_carry(g, n):
                wait(dve, s_scan, lin(g, 2 * NS, 2 * n + 2))
                v.tensor_copy(carry[:, n, :], hb[:, n % 4, :, C - 1]).then_inc(s_car, 1)

            def scan(g, q, n):
                wait(dve, s_dA, lin(g, 2 * NS, 2 * n + 2))
                wait(dve, s_bu, lin(g, NS, n + 1))
                wait(dve, s_hc, lin(g, NS, n - 3))
                if q == 1:
                    if n == 0:
                        wait(dve, s_car, lin(g, NS // 2, NS // 2))
                for h in range(H2):
                    v.tensor_tensor_scan(out=hb[:, n % 4, h], data0=dA[:, n % 4, h], data1=bu[:, n % 2, h],
                                         initial=0.0 if q == 0 else carry[:, n, h:h + 1],
                                         op0=ALU.mult, op1=ALU.add).then_inc(s_scan, 1)

            def post_read(o, q):
                wait(dve, s_gate, lin(o, 1, 0))
                wait(dve, s_o, lin(o, 1, 0))
                wait(dve, s_acc, lin(o, 2 * NS, 2 * NS))
                for h in range(H2):
                    v.scalar_tensor_tensor(out=yg[:, h], in0=xc[:, q, h], scalar=w_D[:, h:h + 1],
                                           in1=acc_ps[h][:, :], op0=ALU.mult, op1=ALU.add).then_inc(s_yg, 1)

            def post_add(o):
                wait(dve, s_o, lin(o, 1, 1))
                xk = X[:, at(o, CT), :]
                v.tensor_tensor(xk, xk, w_ps[1][:, :].rearrange("p (t d) -> p t d", d=D), ALU.add).then_inc(s_x2, 1)

            def window(g, q, a, b, o):
                for n in range(NS):
                    if q == 0 and n >= 1:
                        save_carry(g, n - 1)
                    if n == 2 and o is not None:
                        post_read(o, 1 - q)
                    if n + 1 < NS:
                        dtxb(g, q, n + 1)
                    elif b is not None:
                        dtxb(b, 1 - q, 0)
                    scan(g, q, n)
                    if b is not None:
                        late(b, 1 - q, n)
                    if a is not None:
                        early(a, q, n)
                    if n == 9 and o is not None:
                        post_add(o)
                if q == 0:
                    save_carry(g, NS - 1)

            ffn(0)
            for n in range(NS):
                early(0, 0, n)
            for n in range(NS):
                late(0, 0, n)
                early(1, 1, n)
            dtxb(0, 0, 0)
            window(0, 0, 2, 1, None)
            with dve.Fori(0, LOOPS) as i:
                window((i, 2, 1), 1, (i, 2, 3), (i, 2, 2), (i, 2, 0))
                window((i, 2, 2), 0, (i, 2, 4), (i, 2, 3), (i, 2, 1))
            for g in range(2 * LOOPS + 1, NCH):
                window(g, g % 2, g + 2 if g + 2 < NCH else None, g + 1 if g + 1 < NCH else None, g - 1)
            post_read(NCH - 1, 1)
            post_add(NCH - 1)
            dve.wait_ge(s_x2, NCH)
            ffn(1)


def kernel(**inputs):
    import numpy as np
    import concourse.bacc as bacc
    from concourse.bass_utils import run_bass_kernel_spmd as run

    i = {k: np.asarray(x) for k, x in inputs.items()}
    m = {k[len("L0_attn_"):]: x for k, x in i.items() if k.startswith("L0_attn_")}
    f = {k[len("L0_ffn_"):]: x for k, x in i.items() if k.startswith("L0_ffn_")}

    def halves(w):
        return w.reshape(2, 128, -1).transpose(1, 0, 2)

    arrays = {
        "x": m["resid"].reshape(4096, 128),
        "centT": f["centroids"].T,
        "experts": np.concatenate([
            f["W1"].transpose(2, 0, 1),
            f["W2"].reshape(8, 128, 4, 128).transpose(3, 0, 2, 1).reshape(128, 8, 512),
            f["b1"].reshape(8, 4, 128).transpose(2, 0, 1),
            f["gamma"].T[:, :, None], f["beta"].T[:, :, None]], axis=2),
        "b2": f["b2"],
        "par": np.concatenate([
            halves(m["A_log"]).reshape(128, 32),
            m["conv_b"].reshape(2, 128).T, m["wd2_b"].reshape(2, 128).T, m["W_D"].reshape(2, 128).T,
            m["norm_w"][:, None]], axis=1),
        "in_wT": m["in_w"].T,
        "skip_wT": m["skip_w"].T,
        "conv_wT": m["conv_w"].T,
        "wd2T": m["wd2"].T,
        "wrbcT": halves(np.concatenate([m["wd1"], m["wb"], m["wc"], m["wb"], m["wc"]], axis=0).T),
        "out_wT": halves(m["out_w"].T),
    }
    arrays = {k: np.ascontiguousarray(x) for k, x in arrays.items()}
    nc = bacc.Bacc("TRN2", target_bir_lowering=False, num_devices=1)
    aps = {k: nc.dram_tensor("in_" + k, x.shape, mybir.dt.float32, kind="ExternalInput").ap() for k, x in arrays.items()}
    out = nc.dram_tensor("out_y", (4096, 128), mybir.dt.float32, kind="ExternalOutput").ap()
    build(nc, aps, out)
    r = run(nc, [{"in_" + k: x for k, x in arrays.items()}], core_ids=[0])
    return r.results[0]["out_y"].reshape(4, 1024, 128)
```

```python
from contextlib import ExitStack

import concourse.bass as bass
from concourse import mybir

ALU = mybir.AluOpType
ACT = mybir.ActivationFunctionType
F32 = mybir.dt.float32
BF16 = mybir.dt.bfloat16
I32 = mybir.dt.int32
AX = mybir.AxisListType.X

P = 128
D = 128
E = 8
F = 512
FC = F // P
TOK = 4096
NT = TOK // P
GR = NT // 4
ST = NT + E - 1
WR = 4
XR = 12
YR = 12
AHEAD = 8
PK = F + FC * D + FC + 2 + D
O_W2, O_B1 = F, F + FC * D
O_G, O_B, O_B2 = O_B1 + FC, O_B1 + FC + 1, O_B1 + FC + 2
EPS = 1e-5

H2 = 2
NS = 16
R = 64
TAPS = 4
C = 512
CT = C // P
NCH = TOK // C
HIST = 4
LOOPS = (NCH - 4) // 2
PO = 10
WARM = 14
U = 4
assert NT % 4 == 0 and U % WR == 0


def lin(i, k, c):
    if isinstance(i, tuple):
        reg, a, b = i
        return reg * (a * k) + (b * k + c)
    return k * i + c


def wait(eng, sem, value):
    if not isinstance(value, int) or value > 0:
        eng.wait_ge(sem, value)


def at(i, size, off=0, n=None):
    n = size if n is None else n
    v = lin(i, size, off)
    return slice(v, v + n) if isinstance(v, int) else bass.ds(v, n)


def uses(r, ring):
    return -(-(ST - r) // ring)


def build(nc, a, out):
    with ExitStack() as ctx:
        def sb(name, shape, dt=F32):
            return ctx.enter_context(nc.sbuf_tensor(name, shape, dt))

        def ps(name, shape):
            return ctx.enter_context(nc.psum_tensor(name, shape, F32))

        def sem(name):
            return ctx.enter_context(nc.semaphore(name))

        X = sb("X", [P, NT, D])
        wall = sb("wall", [P, E, PK])
        cent = sb("cent", [D, (2 * GR - 1) * E])
        DA, HB, HC = 4 * H2 * C, 4 * H2 * C, 4 * H2 * C
        XHN, WCN, YSN, XSN = NT * D, WR * PK, YR * D, XR * D
        region = sb("region", [P, max(DA + HB + HC, XHN + WCN + YSN + XSN)])
        xh = region[:, 0:XHN].rearrange("p (t d) -> p t d", d=D)
        back = xh
        wcur = region[:, XHN:XHN + WCN].rearrange("p (r w) -> p r w", w=PK)
        ys = region[:, XHN + WCN:XHN + WCN + YSN].rearrange("p (t d) -> p t d", d=D)
        o = XHN + WCN + YSN
        xs = region[:, o:o + XSN].rearrange("p (t d) -> p t d", d=D)
        dA = region[:, 0:DA].rearrange("p (r h c) -> p r h c", r=4, h=H2)
        hb = region[:, DA:DA + HB].rearrange("p (r h c) -> p r h c", r=4, h=H2)
        hc = region[:, DA + HB:DA + HB + HC].rearrange("p (r h c) -> p r h c", r=4, h=H2)
        xsT = sb("xsT", [D, WR, P])
        stat = sb("stat", [P, NT, 6])
        mom = sb("mom", [P, 4, NT])
        lnin = sb("lnin", [P, 2, NT])
        lnl = sb("lnl", [P, 2, NT])
        rst = sb("rst", [P, 2, NT])
        inv = sb("inv", [P, NT])
        r12 = sb("r12", [P, NT])
        xa = sb("xa", [P, NT])
        xb = sb("xb", [P, NT])
        score = sb("score", [P, NT, E])
        tmpA = sb("tmpA", [P, NT * E])
        tmpB = sb("tmpB", [P, NT * E])
        tot = sb("tot", [P, NT * E])
        oh = sb("oh", [P, E, NT], BF16)
        mx = sb("mx", [P, NT])
        best = sb("best", [P, NT])
        zal = sb("zal", [P, NT])
        eal = sb("eal", [P, NT])
        half_alpha = sb("half_alpha", [P, NT])
        slot_f = sb("slot_f", [P, NT])
        slot = sb("slot", [P, 3, NT], I32)
        slot_tp = sb("slot_tp", [P, 2, NT])
        inv_sb = sb("inv_sb", [P, 5, ST])
        gidx = sb("gidx", [P, ST], I32)
        sidx = sb("sidx", [P, ST], I32)
        small = sb("small", [P, 8, E])
        nti = sb("nti", [P, 2, E], I32)
        cmp = sb("cmp", [P, ST, E])
        texf = sb("texf", [P, ST])
        tex = sb("tex", [P, ST], I32)
        ident = sb("ident", [P, P])
        upper = sb("upper", [P, P], BF16)
        ones_b = sb("ones_b", [P, P], BF16)
        ones_f = sb("ones_f", [P, NT * E])
        desc = sb("desc", [P, E])
        jcon = sb("jcon", [P, ST])
        placecon = sb("placecon", [P, P], BF16)
        tcon = sb("tcon", [P, NT])
        pcon = sb("pcon", [P, 1])
        sparecon = sb("sparecon", [P, ST])
        rowsel = sb("rowsel", [P, 3, 32])
        sel = sb("sel", [P, 32, P], BF16)
        par = sb("par", [P, 2 * NS + 7])
        alog = par[:, 0:2 * NS]
        conv_b = par[:, 2 * NS:2 * NS + 2]
        wd2_b = par[:, 2 * NS + 2:2 * NS + 4]
        w_D = par[:, 2 * NS + 4:2 * NS + 6]
        norm_w = par[:, 2 * NS + 6:2 * NS + 7]
        expA = sb("expA", [P, 2 * NS])
        negA = sb("negA", [P, 2 * NS])
        in_wT = sb("in_wT", [D, H2 * P])
        skip_wT = sb("skip_wT", [D, H2 * P])
        cw = sb("cw", [P, TAPS, H2 * P])
        wd2T = sb("wd2T", [R, H2 * P])
        wrbcT = sb("wrbcT", [P, H2, P])
        out_wT = sb("out_wT", [P, H2, D])
        xr = sb("xr", [P, CT, D])
        xrT = sb("xrT", [D, 2, HIST + C])
        cst = sb("cst", [P, CT, 6])
        cmom = sb("cmom", [P, 4, CT])
        csm = sb("csm", [P, 11, CT])
        xc = sb("xc", [P, 2, H2, C])
        sg = sb("sg", [P, 2, H2, C])
        dt = sb("dt", [P, 2, H2, C])
        u = sb("u", [P, 2, H2, C])
        dtr = sb("dtr", [R, C])
        bcs = sb("bcs", [P, 2, C], BF16)
        bcr = sb("bcr", [P, C])
        sp_t = sb("sp_t", [P, H2, C])
        bu = sb("bu", [P, 2, H2, C])
        cs = sb("cs", [P, 4, C])
        yg = sb("yg", [P, H2, C])
        ftT = yg
        scT = sp_t[0:GR * E, 0, :]
        hT = bu[:, :, :, :].rearrange("p r h c -> p (r h c)")[:, 0:WR * FC * P].rearrange(
            "p (r c t) -> p r c t", r=WR, c=FC)
        place_oh = u[:, :, :, :].rearrange("p r h c -> p (r h c)").bitcast(BF16)[:, 0:NT * P].rearrange(
            "p (t q) -> p t q", q=P)
        tile_oh = dt[:, :, :, :].rearrange("p r h c -> p (r h c)").bitcast(BF16)[:, 0:NT * 3 * ST].rearrange(
            "p (t k j) -> p t k j", k=3, j=ST)
        carry = sb("carry", [P, NS, H2])

        bank = [ps(f"bank{i}", [P, 512]) for i in range(8)]
        tr_ps = [bank[0], bank[1]]
        inv_ps = bank[2][:, 0:2 * ST]
        scT_ps = bank[2][0:GR * E, :]
        sc_ps = bank[4][:, 0:NT * E]
        rank_ps, tot_ps = bank[3][:, 0:NT * E], bank[3][:, NT * E:2 * NT * E]
        xt_ps = [bank[4][:, 0:P], bank[3][:, 0:P]]
        ha_ps = [bank[5], bank[7]]
        hd_ps = [bank[6], bank[2]]
        y_ps = [bank[0][:, 0:D], bank[1][:, 0:D]]
        w_ps = [bank[0], bank[1]]
        b_ps = [bank[2], bank[3]]
        c_ps = [bank[4], bank[5]]
        acc_ps = [bank[6], bank[7]]

        rows_d = nc.dram_tensor("normed_rows", [TOK, D], F32, kind="Internal").ap()
        res_d = nc.dram_tensor("results", [TOK + ST * P, D], F32, kind="Internal").ap()
        rows_v = rows_d.rearrange("(t p) d -> p t d", p=P)
        res_v = res_d[0:TOK, :].rearrange("(t p) d -> p t d", p=P)
        x_v = a["x"].rearrange("(t p) d -> p t d", p=P)
        out_v = out.rearrange("(t p) d -> p t d", p=P)

        s_x = [sem(f"x_loaded{i}") for i in range(GR)]
        s_par = sem("params_loaded")
        s_w = sem("expert_weights_loaded")
        s_cent = sem("centroids_loaded")
        s_rows = sem("normed_stored")
        s_pc = sem("pool_consts")
        s_dc = sem("mamba_consts")
        s_ea = sem("exp_a_log")
        own = sem("dve_chain")
        s_lnin = sem("variances_ready")
        s_lnl = sem("logs_ready")
        s_rst = sem("rstd_ready")
        s_xh = sem("normed_ready")
        s_trA = sem("normed_transposed")
        s_ftT = sem("normedT_copied")
        s_sc = sem("scores_done")
        s_scT = sem("scores_copied")
        s_sct = sem("scores_transposed")
        s_z = sem("alpha_arg_ready")
        s_ez = sem("alpha_exp_done")
        s_oh = sem("onehot_ready")
        s_rank = sem("ranks_done")
        s_place = sem("place_onehots_ready")
        s_placeP = sem("place_onehots_pool")
        s_slot = sem("slots_ready")
        s_inv = sem("slots_turned_round")
        s_idx = sem("indices_ready")
        s_xs = [sem(f"gathered{i}") for i in range(XR)]
        s_xt = sem("sorted_transposed")
        s_xsT = sem("sortedT_copied")
        s_wc = sem("weights_current")
        s_h = sem("hidden_done")
        s_ra = sem("relu_act_done")
        s_rd = sem("relu_dve_done")
        s_y = sem("result_done")
        s_ys = sem("result_copied")
        s_yst = [sem(f"scattered{i}") for i in range(YR)]
        s_g = [sem(f"results_loaded{i}") for i in range(GR)]
        s_aff = sem("x_scaled")
        s_x1 = sem("ffn_residual_added")
        s_out = sem("output_stored")
        s_cln = sem("m_variances_ready")
        s_cl = sem("m_logs_ready")
        s_cr = sem("m_rstd_ready")
        s_nb = sem("m_scale_bias_ready")
        s_xr = sem("m_normed_ready")
        s_u0 = sem("m_transposed")
        s_xrT = sem("m_normedT_copied")
        s_hist = sem("m_history_copied")
        s_conv = sem("m_conv_done")
        s_skip = sem("m_skip_done")
        s_xc = sem("m_x_ready")
        s_sg = sem("m_gate_ready")
        s_rbc = sem("m_dtrank_bc_done")
        s_dtc = sem("m_dtrank_copied")
        s_hi = sem("m_bc_high_part")
        s_split = sem("m_bc_split")
        s_zz = sem("m_dtarg_done")
        s_abs = sem("m_dtarg_abs")
        s_ex = sem("m_softplus_exp")
        s_sp = sem("m_softplus_log")
        s_rz = sem("m_dtarg_relu")
        s_dt = sem("m_dt_ready")
        s_u = sem("m_dtx_ready")
        s_b = sem("m_b_broadcast")
        s_c = sem("m_c_broadcast")
        s_cs = sem("m_c_copied")
        s_dA = sem("m_decay_ready")
        s_bu = sem("m_dtxb_ready")
        s_scan = sem("m_scanned")
        s_car = sem("m_carry_saved")
        s_hc = sem("m_hc_ready")
        s_acc = sem("m_summed")
        s_yg = sem("m_y_read")
        s_gate = sem("m_gated")
        s_o = sem("m_projected")
        s_x2 = sem("m_residual_added")
        s_res = sem("m_residual_scaled")
        s_stat = sem("statistics_ready")
        s_own2 = sem("m_norm_chain")
        s_own3 = sem("m_split_chain")

        block = ctx.enter_context(nc.Block())

        @block.sync
        def _(sp):
            for g in range(GR):
                sp.dma_start(X[:, 4 * g:4 * g + 4, :], x_v[:, 4 * g:4 * g + 4, :]).then_inc(s_x[g], 16)
            sp.dma_start(cent[:, (GR - 1) * E:GR * E], a["centT"]).then_inc(s_cent, 16)
            for dst, src in ((par, "par"), (in_wT, "in_wT"), (skip_wT, "skip_wT"), (wd2T, "wd2T")):
                sp.dma_start(dst[:, :], a[src]).then_inc(s_par, 16)
            for dst, src in ((wrbcT, "wrbcT"), (out_wT, "out_wT")):
                sp.dma_start(dst[:, :, :], a[src]).then_inc(s_par, 16)
            sp.dma_start(cw[:, :, :], a["conv_wT"].partition_broadcast(P)).then_inc(s_par, 16)

            for f in range(2):
                for g in range(GR):
                    sp.wait_ge(s_xh, NT * f + 4 * (g + 1))
                    sp.dma_start(rows_v[:, 4 * g:4 * g + 4, :], xh[:, 4 * g:4 * g + 4, :]).then_inc(s_rows, 16)
                if f == 0:
                    sp.dma_start(wall[:, :, 0:O_B2], a["experts"]).then_inc(s_w, 16)
                    sp.dma_start(wall[:, :, O_B2:PK], a["b2"].partition_broadcast(P)).then_inc(s_w, 16)
                for r in range(YR):
                    sp.wait_ge(s_yst[r], 16 * uses(r, YR) * (f + 1))
                for g in range(GR):
                    sp.dma_start(back[:, 4 * g:4 * g + 4, :], res_v[:, 4 * g:4 * g + 4, :]).then_inc(s_g[g], 16)
            for g in range(GR):
                sp.wait_ge(s_x1, NT + 4 * (g + 1))
                sp.dma_start(out_v[:, 4 * g:4 * g + 4, :], X[:, 4 * g:4 * g + 4, :]).then_inc(s_out, 16)
            sp.wait_ge(s_out, 16 * GR)

        @block.gpsimd
        def _(pool):
            pool.memset(ident[:, :], 0.0).then_inc(s_pc, 1)
            pool.memset(upper[:, :], 0.0).then_inc(s_pc, 1)
            pool.memset(ones_b[:, :], 1.0).then_inc(s_pc, 1)
            pool.memset(ones_f[:, :], 1.0).then_inc(s_pc, 1)
            pool.memset(xrT[:, 0, 0:HIST], 0.0).then_inc(s_pc, 1)
            pool.memset(cent[:, 0:(GR - 1) * E], 0.0).then_inc(s_pc, 1)
            pool.memset(cent[:, GR * E:(2 * GR - 1) * E], 0.0).then_inc(s_pc, 1)
            pool.wait_ge(s_pc, 7)
            pool.affine_select(out=ident[:, :], in_=ident[:, :], compare_op=ALU.not_equal, fill=1.0,
                               base=0, pattern=[[-1, P]], channel_multiplier=1).then_inc(s_pc, 1)
            pool.affine_select(out=upper[:, :], in_=upper[:, :], compare_op=ALU.is_ge, fill=1.0,
                               base=0, pattern=[[-1, P]], channel_multiplier=1).then_inc(s_pc, 1)
            pool.iota(desc[:, :], pattern=[[-1, E]], base=E, channel_multiplier=0,
                      allow_small_or_imprecise_dtypes=True).then_inc(s_pc, 1)
            for con, n, step, base, mult in ((jcon, ST, 1, 0, 0), (placecon, P, 1, 0, 0), (tcon, NT, 1, 0, 0),
                                             (pcon, 1, 0, 1, 1), (sparecon, ST, P, TOK + 1, 1)):
                pool.iota(con[:, :], pattern=[[step, n]], base=base, channel_multiplier=mult,
                          allow_small_or_imprecise_dtypes=True).then_inc(s_pc, 1)

            def route(f):
                pool.wait_ge(s_slot, f + 1)
                for t in range(NT - PO, NT):
                    pool.tensor_scalar(place_oh[:, t, :], placecon[:, :], slot_tp[:, 1, t:t + 1], None,
                                       ALU.is_equal).then_inc(s_placeP, 1)
                pool.wait_ge(s_rows, 16 * GR * (f + 1))
                pool.wait_ge(s_idx, f + 1)

                def gather(j):
                    r = j % XR
                    wait(pool, s_xt, ST * f + j - XR + 1)
                    pool.indirect_dma_start(xs[:, r, :], None, rows_d,
                                            bass.IndirectOffsetOnAxis(ap=gidx[:, j:j + 1], axis=0)
                                            ).then_inc(s_xs[r], 16)

                def scatter(j):
                    r = j % YR
                    pool.wait_ge(s_ys, ST * f + j + 1)
                    pool.indirect_dma_start(res_d, bass.IndirectOffsetOnAxis(ap=sidx[:, j:j + 1], axis=0),
                                            ys[:, r, :], None).then_inc(s_yst[r], 16)

                for j in range(AHEAD):
                    gather(j)
                for j in range(ST):
                    if j + AHEAD < ST:
                        gather(j + AHEAD)
                    scatter(j)

            def gate(o, par_):
                wait(pool, s_yg, lin(o, 2, 2))
                wait(pool, s_sg, lin(o, 2, 2))
                pool.tensor_tensor(yg[:, :, :], yg[:, :, :], sg[:, par_], ALU.mult).then_inc(s_gate, 1)

            def window(g, par_, post):
                for n in range(NS):
                    wait(pool, s_scan, lin(g, 2 * NS, 2 * n + 2))
                    wait(pool, s_cs, lin(g, NS, n + 1))
                    wait(pool, s_acc, lin(g, 2 * NS, 2 * (n - 4) + 2))
                    pool.tensor_tensor(hc[:, n % 4], hb[:, n % 4],
                                       cs[:, n % 4].unsqueeze(1).broadcast_to([P, H2, C]),
                                       ALU.mult).then_inc(s_hc, 1)
                    if n == 3 and post is not None:
                        gate(post, 1 - par_)

            pool.memset(bcs[:, :, :], 0.0).then_inc(s_dc, 1)
            pool.wait_ge(s_pc, 15)
            rs = ident[:, :].rearrange("p (j n) -> p j n", j=4)
            pool.tensor_tensor(rowsel[:, 0, :], rs[:, 0], rs[:, 1], ALU.add).then_inc(s_dc, 1)
            pool.tensor_tensor(rowsel[:, 1, :], rs[:, 2], rs[:, 3], ALU.add).then_inc(s_dc, 1)
            pool.wait_ge(s_dc, 3)
            pool.tensor_tensor(rowsel[:, 2, :], rowsel[:, 0, :], rowsel[:, 1, :], ALU.add).then_inc(s_dc, 1)
            pool.wait_ge(s_dc, 4)
            for k in range(4):
                pool.tensor_copy(sel[:, 8 * k:8 * k + 8, :],
                                 rowsel[:, 2, 8 * k:8 * k + 8].unsqueeze(2).broadcast_to([P, 8, P])
                                 ).then_inc(s_dc, 1)
            pool.wait_ge(s_par, 16 * 7)
            pool.wait_ge(s_ea, 1)
            pool.tensor_scalar(negA[:, :], expA[:, :], -1.0, None, ALU.mult).then_inc(s_dc, 1)
            pool.tensor_scalar(in_wT[:, :], in_wT[:, :], norm_w, None, ALU.mult).then_inc(s_dc, 1)
            pool.tensor_scalar(skip_wT[:, :], skip_wT[:, :], norm_w, None, ALU.mult).then_inc(s_dc, 1)
            pool.wait_ge(s_dc, 11)
            for k in range(TAPS):
                pool.tensor_tensor(cw[:, k], cw[:, k], in_wT[:, :], ALU.mult).then_inc(s_dc, 1)
            route(0)
            window(0, 0, None)
            with pool.Fori(0, LOOPS) as i:
                window((i, 2, 1), 1, (i, 2, 0))
                window((i, 2, 2), 0, (i, 2, 1))
            for g in range(2 * LOOPS + 1, NCH):
                window(g, g % 2, g - 1)
            gate(NCH - 1, 1)
            route(1)

        @block.scalar
        def _(act):
            nc.scalar.preload_act_table_set("natural_log_exp_and_others")

            def ffn(f):
                act.wait_ge(s_lnin, f + 1)
                nc.scalar.activation(lnl[:, :, :], lnin[:, :, :], ACT.Ln).then_inc(s_lnl, 1)
                act.wait_ge(s_lnl, f + 1)
                nc.scalar.activation(rst[:, :, :], lnl[:, :, :], ACT.Exp, scale=-0.5).then_inc(s_rst, 1)
                for g in range(GR):
                    act.wait_ge(s_trA, GR * f + g + 1)
                    if g >= 2:
                        act.wait_ge(s_sc, GR * f + g - 1)
                    nc.scalar.activation(ftT[:, g % 2], tr_ps[g % 2][:, :], ACT.Copy).then_inc(s_ftT, 1)
                act.wait_ge(s_sc, GR * (f + 1))
                nc.scalar.activation(scT, scT_ps, ACT.Copy).then_inc(s_scT, 1)
                if f == 0:
                    act.wait_ge(s_par, 16 * 7)
                    nc.scalar.activation(expA[:, :], alog, ACT.Exp).then_inc(s_ea, 1)
                act.wait_ge(s_z, f + 1)
                nc.scalar.activation(eal[:, :], zal[:, :], ACT.Exp, scale=-1.0).then_inc(s_ez, 1)

                def tile(j, s):
                    wait(act, s_xt, lin(j, 1, ST * f + 1))
                    wait(act, s_wc, lin(j, 1, ST * f + 1))
                    wait(act, s_h, lin(j, 1, ST * f + 1 - WR))
                    nc.scalar.activation(xsT[:, s % WR], xt_ps[s % 2], ACT.Identity,
                                         scale=wcur[:, s % WR, O_G:O_G + 1],
                                         bias=wcur[:, s % WR, O_B:O_B + 1]).then_inc(s_xsT, 1)

                def relu(j, s):
                    wait(act, s_h, lin(j, 1, ST * f + 1))
                    wait(act, s_y, lin(j, 1, ST * f + 1 - WR))
                    for c in (0, 1):
                        nc.scalar.activation(hT[:, s % WR, c], ha_ps[s % 2][:, P * c:P * c + P], ACT.Relu,
                                             bias=wcur[:, s % WR, O_B1 + c:O_B1 + c + 1]).then_inc(s_ra, 1)

                tile(0, 0)
                for j in range(U):
                    tile(j + 1, j + 1)
                    relu(j, j)
                with act.Fori(1, ST // U) as i:
                    for s in range(U):
                        tile((i, U, s + 1), s + 1)
                        relu((i, U, s), s)
                for j in range(ST // U * U, ST):
                    if j + 1 < ST:
                        tile(j + 1, j + 1)
                    relu(j, j)

            def prep_norm(p):
                wait(act, s_cln, lin(p, 1, 1))
                nc.scalar.activation(csm[:, 2:4, :], csm[:, 0:2, :], ACT.Ln).then_inc(s_cl, 1)
                wait(act, s_cl, lin(p, 1, 1))
                nc.scalar.activation(csm[:, 4:6, :], csm[:, 2:4, :], ACT.Exp, scale=-0.5).then_inc(s_cr, 1)

            def prep_xr(p):
                wait(act, s_nb, lin(p, 1, 1))
                wait(act, s_u0, lin(p, 1, 0))
                for k in range(CT):
                    ins = nc.scalar.activation(xr[:, k, :], X[:, at(p, CT, k, 1), :].rearrange("p o d -> p (o d)"),
                                               ACT.Identity, scale=csm[:, 7, k:k + 1], bias=csm[:, 10, k:k + 1])
                ins.then_inc(s_xr, 1)

            def prep_res(p):
                for k in range(CT):
                    xk = X[:, at(p, CT, k, 1), :].rearrange("p o d -> p (o d)")
                    ins = nc.scalar.activation(xk, xk, ACT.Identity, scale=csm[:, 9, k:k + 1], bias=csm[:, 8, k:k + 1])
                ins.then_inc(s_res, 1)

            def prep_xrT(p, q):
                wait(act, s_u0, lin(p, 1, 1))
                nc.scalar.activation(xrT[:, q, HIST:HIST + C], w_ps[0][:, :], ACT.Copy).then_inc(s_xrT, 1)
                if q == 1:
                    nc.scalar.activation(xrT[:, 1, 0:HIST], xrT[:, 0, C:C + HIST], ACT.Copy).then_inc(s_hist, 1)

            def prep_silu(p, q):
                for h in range(H2):
                    wait(act, s_conv, lin(p, 2, h + 1))
                    wait(act, s_yg, lin(p, 2, -2))
                    nc.scalar.activation(xc[:, q, h], w_ps[1 - h][:, :], ACT.Silu,
                                         bias=conv_b[:, h:h + 1]).then_inc(s_xc, 1)
                for h in range(H2):
                    wait(act, s_skip, lin(p, 2, h + 1))
                    wait(act, s_gate, lin(p, 1, -1))
                    nc.scalar.activation(sg[:, q, h], w_ps[1 - h][:, :], ACT.Silu).then_inc(s_sg, 1)
                nc.scalar.preload_act_table_set("natural_log_exp_and_others")

            def prep_rbc(p, q):
                wait(act, s_rbc, lin(p, 1, 1))
                wait(act, s_zz, lin(p, 2, 0))
                nc.scalar.activation(bcs[64:128, q], w_ps[0][64:128, :], ACT.Copy).then_inc(s_hi, 1)
                nc.scalar.activation(dtr[:, :], w_ps[0][0:R, :], ACT.Copy).then_inc(s_dtc, 1)

            def prep_softplus(p):
                for h in range(H2):
                    wait(act, s_zz, lin(p, 2, h + 1))
                    wait(act, s_dt, lin(p, 2, h - 1))
                    nc.scalar.activation(sp_t[:, h], w_ps[h][:, :], ACT.Abs,
                                         bias=wd2_b[:, h:h + 1]).then_inc(s_abs, 1)
                for h in range(H2):
                    wait(act, s_abs, lin(p, 2, h + 1))
                    nc.scalar.activation(sp_t[:, h], sp_t[:, h], ACT.Exp, scale=-1.0).then_inc(s_ex, 1)
                for h in range(H2):
                    wait(act, s_ex, lin(p, 2, h + 1))
                    nc.scalar.activation(sp_t[:, h], sp_t[:, h], ACT.Ln, bias=1.0).then_inc(s_sp, 1)

            def decay(g, q, n):
                if n == 0:
                    wait(act, s_dt, lin(g, 2, 2))
                wait(act, s_scan, lin(g, 2 * NS, 2 * (n - 4) + 2))
                for h in range(H2):
                    nc.scalar.activation(dA[:, n % 4, h], dt[:, q, h], ACT.Exp,
                                         scale=negA[:, h * NS + n:h * NS + n + 1]).then_inc(s_dA, 1)

            def copy_c(g, n):
                wait(act, s_c, lin(g, NS, n + 1))
                wait(act, s_hc, lin(g, NS, n - 3))
                nc.scalar.activation(cs[:, n % 4], c_ps[n % 2][:, :], ACT.Copy).then_inc(s_cs, 1)

            def early(a, q, n):
                if n == 8:
                    prep_norm(a)
                if n == 10:
                    prep_xr(a)
                if n == 12:
                    prep_xrT(a, q)
                if n == 14:
                    prep_res(a)

            def late(b, q, n):
                if n == 4:
                    prep_silu(b, q)
                if n == 6:
                    prep_rbc(b, q)
                if n == 11:
                    prep_softplus(b)

            def window(g, q, a, b):
                for n in range(NS):
                    if n + 2 < NS:
                        decay(g, q, n + 2)
                    elif b is not None:
                        decay(b, 1 - q, n + 2 - NS)
                    if n + 1 < NS:
                        copy_c(g, n + 1)
                    elif b is not None:
                        copy_c(b, 0)
                    if b is not None:
                        late(b, 1 - q, n)
                    if a is not None:
                        early(a, q, n)

            ffn(0)
            act.wait_ge(s_dc, 15)
            for n in range(NS):
                early(0, 0, n)
            for n in range(NS):
                late(0, 0, n)
                early(1, 1, n)
            decay(0, 0, 0)
            decay(0, 0, 1)
            copy_c(0, 0)
            window(0, 0, 2, 1)
            with act.Fori(0, LOOPS) as i:
                window((i, 2, 1), 1, (i, 2, 3), (i, 2, 2))
                window((i, 2, 2), 0, (i, 2, 4), (i, 2, 3))
            for g in range(2 * LOOPS + 1, NCH):
                window(g, g % 2, g + 2 if g + 2 < NCH else None, g + 1 if g + 1 < NCH else None)
            ffn(1)

        @block.tensor
        def _(pe):
            mm = nc.tensor.matmul

            def warm(n):
                for _ in range(n):
                    mm(bank[7][:, 0:P], ident[:, :], ident[:, :], start=True, stop=True)

            def ffn(f):
                pe.wait_ge(s_pc, 15)
                if f == 0:
                    pe.wait_ge(s_cent, 16)

                def scores(g):
                    pe.wait_ge(s_ftT, GR * f + g + 1)
                    mm(scT_ps, cent[:, (GR - 1 - g) * E:(2 * GR - 1 - g) * E], ftT[:, g % 2, :],
                       start=(g == 0), stop=(g == GR - 1)).then_inc(s_sc, 1)

                for g in range(GR):
                    pe.wait_ge(s_xh, NT * f + 4 * (g + 1))
                    if g >= 2:
                        pe.wait_ge(s_ftT, GR * f + g - 1)
                    for k in range(4):
                        last = nc.tensor.transpose(tr_ps[g % 2][:, P * k:P * k + P], xh[:, 4 * g + k, :], ident[:, :])
                    last.then_inc(s_trA, 1)
                    if g >= 1:
                        scores(g - 1)
                scores(GR - 1)
                pe.wait_ge(s_scT, f + 1)
                for k in range(4):
                    last = nc.tensor.transpose(sc_ps[:, GR * E * k:GR * E * (k + 1)], scT[:, P * k:P * k + P],
                                               ident[0:GR * E, 0:GR * E])
                last.then_inc(s_sct, 1)
                pe.wait_ge(s_oh, f + 1)
                oh_v = oh[:, :, :].rearrange("p e t -> p (e t)")
                mm(rank_ps, upper[:, :], oh_v, start=True, stop=True)
                mm(tot_ps, ones_b[:, :], oh_v, start=True, stop=True).then_inc(s_rank, 1)

                pe.wait_ge(s_placeP, PO * (f + 1))
                for t in range(NT):
                    if t < NT - PO:
                        pe.wait_ge(s_place, (NT - PO) * f + t + 1)
                    last = mm(inv_ps, place_oh[:, t, :], tile_oh[:, t, 0:2, :].rearrange("p k j -> p (k j)"),
                              start=(t == 0), stop=(t == NT - 1))
                last.then_inc(s_inv, 1)
                warm(WARM)

                def transpose(j):
                    pe.wait_ge(s_xs[j % XR], 16 * (uses(j % XR, XR) * f + j // XR + 1))
                    wait(pe, s_xsT, ST * f + j - 1)
                    nc.tensor.transpose(xt_ps[j % 2], xs[:, j % XR, :], ident[:, :]).then_inc(s_xt, 1)

                def hidden(j):
                    pe.wait_ge(s_wc, ST * f + j + 1)
                    pe.wait_ge(s_xsT, ST * f + j + 1)
                    wait(pe, s_ra, 2 * (ST * f + j) - 2)
                    wait(pe, s_rd, 2 * (ST * f + j) - 2)
                    for c in range(FC):
                        to = (ha_ps if c < 2 else hd_ps)[j % 2]
                        last = mm(to[:, P * (c % 2):P * (c % 2) + P], wcur[:, j % WR, P * c:P * c + P],
                                  xsT[:, j % WR], start=True, stop=True)
                    last.then_inc(s_h, 1)

                def result(j):
                    pe.wait_ge(s_ra, 2 * (ST * f + j) + 2)
                    pe.wait_ge(s_rd, 2 * (ST * f + j) + 2)
                    wait(pe, s_ys, ST * f + j - 1)
                    for c in range(FC):
                        last = mm(y_ps[j % 2], hT[:, j % WR, c],
                                  wcur[:, j % WR, O_W2 + D * c:O_W2 + D * c + D],
                                  start=(c == 0), stop=(c == FC - 1))
                    last.then_inc(s_y, 1)

                transpose(0)
                for j in range(ST):
                    if j + 1 < ST:
                        transpose(j + 1)
                    hidden(j)
                    if j >= 1:
                        result(j - 1)
                result(ST - 1)

            def p_transpose(p):
                wait(pe, s_xr, lin(p, 1, 1))
                wait(pe, s_rz, lin(p, 2, -1))
                wait(pe, s_abs, lin(p, 2, -1))
                for k in range(CT):
                    last = nc.tensor.transpose(w_ps[0][:, P * k:P * k + P], xr[:, k, :], ident[:, :])
                last.then_inc(s_u0, 1)

            def p_conv(p, q, h, taps):
                if 0 in taps:
                    wait(pe, s_xrT, lin(p, 1, 1))
                    if q == 1:
                        wait(pe, s_hist, lin(p, 1, 1) // 2 if isinstance(p, int) else lin((p[0], 1, (p[2] + 1) // 2), 1, 0))
                    if h == 0:
                        wait(pe, s_rz, lin(p, 2, 0))
                        wait(pe, s_abs, lin(p, 2, 0))
                        wait(pe, s_x2, lin(p, 1, -2))
                for k in taps:
                    o = HIST - (TAPS - 1) + k
                    last = mm(w_ps[1 - h][:, :], cw[:, k, P * h:P * h + P], xrT[:, q, o:o + C],
                              start=(k == 0), stop=(k == TAPS - 1))
                if TAPS - 1 in taps:
                    last.then_inc(s_conv, 1)

            def p_skip(p, q, h):
                wait(pe, s_xc, lin(p, 2, h + 1))
                mm(w_ps[1 - h][:, :], skip_wT[:, P * h:P * h + P], xrT[:, q, HIST:HIST + C],
                   start=True, stop=True).then_inc(s_skip, 1)

            def p_rbc(p, q, h):
                if h == 0:
                    wait(pe, s_sg, lin(p, 2, 2))
                last = mm(w_ps[0][:, :], wrbcT[:, h], xc[:, q, h], start=(h == 0), stop=(h == 1))
                if h == 1:
                    last.then_inc(s_rbc, 1)

            def p_z(p, h):
                if h == 0:
                    wait(pe, s_dtc, lin(p, 1, 1))
                    wait(pe, s_split, lin(p, 1, 1))
                else:
                    wait(pe, s_x2, lin(p, 1, -1))
                mm(w_ps[h][:, :], wd2T[:, P * h:P * h + P], dtr[:, :], start=True, stop=True).then_inc(s_zz, 1)

            def bcast(g, q, n):
                if n == 0:
                    wait(pe, s_split, lin(g, 1, 1))
                wait(pe, s_bu, lin(g, NS, n - 1))
                mm(b_ps[n % 2][:, :], sel[:, n], bcs[:, q], start=True, stop=True).then_inc(s_b, 1)
                wait(pe, s_cs, lin(g, NS, n - 1))
                mm(c_ps[n % 2][:, :], sel[:, NS + n], bcs[:, q], start=True, stop=True).then_inc(s_c, 1)

            def summed(g, n):
                wait(pe, s_hc, lin(g, NS, n + 1))
                if n == 0:
                    wait(pe, s_yg, lin(g, 2, 0))
                for h in range(H2):
                    mm(acc_ps[h][:, :], ident[:, :], hc[:, n % 4, h], start=(n == 0), stop=(n == NS - 1),
                       ).then_inc(s_acc, 1)

            def project(o, tiles):
                if 0 in tiles:
                    wait(pe, s_gate, lin(o, 1, 1))
                for k in tiles:
                    for h in range(H2):
                        last = mm(w_ps[1][:, P * k:P * k + P], yg[:, h, P * k:P * k + P], out_wT[:, h],
                                  start=(h == 0), stop=(h == 1))
                if CT - 1 in tiles:
                    last.then_inc(s_o, 1)

            def early(a, q, n):
                if n == 12:
                    p_transpose(a)
                if n >= 13:
                    p_conv(a, q, 0, ((0,), (1,), (2, 3))[n - 13])

            def late(b, q, n):
                if n < 4:
                    p_conv(b, q, 1, (n,))
                if n == 4:
                    p_skip(b, q, 0)
                    p_skip(b, q, 1)
                if n in (5, 6):
                    p_rbc(b, q, n - 5)
                if n in (10, 11):
                    p_z(b, n - 10)

            def window(g, q, a, b, o):
                for n in range(NS):
                    if n == 0 and o is None:
                        pass
                    elif n + 1 < NS:
                        bcast(g, q, n + 1)
                    elif b is not None:
                        bcast(b, 1 - q, 0)
                    if n >= 2:
                        summed(g, n - 2)
                    elif o is not None:
                        summed(o, NS + n - 2)
                    if b is not None:
                        late(b, 1 - q, n)
                    if o is not None and n in (8, 9):
                        if b is None:
                            wait(pe, s_rz, lin(g, 2, 2))
                            wait(pe, s_abs, lin(g, 2, 2))
                        project(o, (0, 1) if n == 8 else (2, 3))
                    if a is not None:
                        early(a, q, n)

            ffn(0)
            pe.wait_ge(s_dc, 15)
            pe.wait_ge(s_g[0], 16)
            warm(20)
            for n in range(NS):
                early(0, 0, n)
            for n in range(NS):
                late(0, 0, n)
                if n == 6:
                    warm(14)
                if n == 12:
                    bcast(0, 0, 0)
                    bcast(0, 0, 1)
                early(1, 1, n)
            window(0, 0, 2, 1, None)
            with pe.Fori(0, LOOPS) as i:
                window((i, 2, 1), 1, (i, 2, 3), (i, 2, 2), (i, 2, 0))
                window((i, 2, 2), 0, (i, 2, 4), (i, 2, 3), (i, 2, 1))
            for g in range(2 * LOOPS + 1, NCH):
                window(g, g % 2, g + 2 if g + 2 < NCH else None, g + 1 if g + 1 < NCH else None, g - 1)
            summed(NCH - 1, NS - 2)
            summed(NCH - 1, NS - 1)
            pe.wait_ge(s_x2, NCH - 1)
            project(NCH - 1, range(CT))
            ffn(1)

        @block.vector
        def _(dve):
            v = nc.vector
            chain = [0]

            def link(ins):
                chain[0] += 1
                ins.then_inc(own, 1)
                dve.wait_ge(own, chain[0])

            def bc(ap, axis, shape):
                return ap.unsqueeze(axis).broadcast_to(shape)

            def moments(st, m):
                half = D // 2
                v.tensor_tensor(m[:, 0], st[:, :, 1], st[:, :, 4], ALU.add)
                v.tensor_tensor(m[:, 1], st[:, :, 1], st[:, :, 4], ALU.subtract)
                yield v.tensor_tensor(m[:, 2], st[:, :, 2], st[:, :, 5], ALU.add)
                v.tensor_scalar(m[:, 0], m[:, 0], 0.5, None, ALU.mult)
                v.tensor_scalar(m[:, 2], m[:, 2], 0.5 / half, None, ALU.mult)
                yield v.scalar_tensor_tensor(out=m[:, 1], in0=m[:, 1], scalar=0.25, in1=m[:, 1],
                                             op0=ALU.mult, op1=ALU.mult)
                yield v.tensor_tensor(m[:, 3], m[:, 1], m[:, 2], ALU.add)

            def ffn(f):
                if f == 0:
                    for t in range(NT):
                        if t % 4 == 0:
                            dve.wait_ge(s_x[t // 4], 16)
                        last = v.bn_stats(stat[:, t, :], X[:, t, :])
                    link(last)
                else:
                    dve.wait_ge(s_stat, NCH)
                for part in moments(stat, mom):
                    link(part)
                mean, var = mom[:, 0], mom[:, 3]
                link(v.tensor_scalar(lnin[:, 0], var, EPS, None, ALU.add))
                link(v.reciprocal(inv[:, :], lnin[:, 0]))
                link(v.tensor_tensor(lnin[:, 1], var, inv[:, :], ALU.mult))
                v.tensor_scalar(lnin[:, 1], lnin[:, 1], EPS, None, ALU.add).then_inc(s_lnin, 1)
                dve.wait_ge(s_rst, f + 1)
                link(v.tensor_tensor(r12[:, :], rst[:, 0], rst[:, 1], ALU.mult))
                for t in range(NT):
                    v.tensor_scalar(xh[:, t, :], X[:, t, :], mean[:, t:t + 1], r12[:, t:t + 1],
                                    ALU.subtract, ALU.mult).then_inc(s_xh, 1)
                link(v.tensor_scalar(xa[:, :], rst[:, 0], 0.5, None, ALU.mult))
                link(v.tensor_tensor(xb[:, :], xa[:, :], mean, ALU.mult))
                link(v.tensor_scalar(xa[:, :], xa[:, :], 1.0, None, ALU.add))
                dve.wait_ge(s_sct, f + 1)
                link(v.tensor_copy(score[:, :, :].rearrange("p (g k) e -> p g k e", k=4),
                                   sc_ps.rearrange("p (k g e) -> p g k e", g=GR, e=E)))
                link(v.tensor_reduce(mx[:, :], score[:, :, :], AX, ALU.max))
                cand = tmpA[:, :].rearrange("p (t e) -> p t e", e=E)
                link(v.tensor_tensor(cand, score[:, :, :], bc(mx[:, :], 2, [P, NT, E]), ALU.is_equal))
                link(v.tensor_tensor(cand, cand, bc(desc[:, :], 1, [P, NT, E]), ALU.mult))
                link(v.tensor_reduce(best[:, :], cand, AX, ALU.max))
                v.tensor_tensor(oh[:, :, :].rearrange("p e t -> p t e"), cand, bc(best[:, :], 2, [P, NT, E]),
                                ALU.is_equal).then_inc(s_oh, 1)
                link(v.tensor_tensor(zal[:, :], mx[:, :], lnin[:, 1], ALU.mult))
                v.tensor_tensor(zal[:, :], zal[:, :], rst[:, 1], ALU.mult).then_inc(s_z, 1)
                dve.wait_ge(s_rank, f + 1)
                link(v.tensor_copy(tot[:, :], tot_ps))
                link(v.tensor_tensor_scan(out=tmpA[:, :], data0=ones_f[:, :], data1=tot[:, :], initial=0.0,
                                          op0=ALU.mult, op1=ALU.add))
                ends = tmpA[:, :].rearrange("p (e t) -> p e t", t=NT)[:, :, NT - 1]
                link(v.tensor_reduce(small[:, 0], tot[:, :].rearrange("p (e t) -> p e t", t=NT), AX, ALU.add))
                link(v.tensor_tensor(small[:, 1], ends, small[:, 0], ALU.subtract))
                link(v.tensor_tensor(tmpB[:, :], tmpA[:, :], tot[:, :], ALU.subtract))
                link(v.tensor_scalar(nti[:, 0], small[:, 0], float(P - 1), None, ALU.add))
                link(v.tensor_scalar(nti[:, 1], nti[:, 0], P.bit_length() - 1, None, ALU.logical_shift_right))
                link(v.tensor_copy(small[:, 2], nti[:, 1]))
                link(v.tensor_tensor_scan(out=small[:, 3], data0=ones_f[:, 0:E], data1=small[:, 2], initial=0.0,
                                          op0=ALU.mult, op1=ALU.add))
                link(v.tensor_tensor(small[:, 4], small[:, 3], small[:, 2], ALU.subtract))
                link(v.scalar_tensor_tensor(out=small[:, 5], in0=small[:, 4], scalar=float(P), in1=small[:, 1],
                                            op0=ALU.mult, op1=ALU.subtract))
                link(v.tensor_tensor(tmpB[:, :], tmpB[:, :], rank_ps, ALU.add))
                pos = tmpB[:, :].rearrange("p (e t) -> p e t", t=NT)
                link(v.tensor_tensor(pos, pos, bc(small[:, 5], 2, [P, E, NT]), ALU.add))
                link(v.tensor_tensor(pos, pos, oh[:, :, :], ALU.mult))
                link(v.tensor_reduce(slot_f[:, :], pos.rearrange("p e t -> p t e"), AX, ALU.add))
                link(v.tensor_copy(slot[:, 0], slot_f[:, :]))
                v.tensor_scalar(slot[:, 1], slot[:, 0], P.bit_length() - 1, None, ALU.logical_shift_right)
                link(v.tensor_scalar(slot[:, 2], slot[:, 0], P - 1, None, ALU.bitwise_and))
                v.tensor_copy(slot_tp[:, :, :], slot[:, 1:3, :]).then_inc(s_slot, 1)
                dve.wait_ge(s_slot, f + 1)
                link(v.tensor_tensor(tile_oh[:, :, 2], bc(slot_tp[:, 0], 2, [P, NT, ST]),
                                     bc(jcon[:, :], 1, [P, NT, ST]), ALU.is_equal))
                v.tensor_scalar(tile_oh[:, :, 0], tile_oh[:, :, 2], pcon[:, 0:1], None, ALU.mult)
                link(v.tensor_tensor(tile_oh[:, :, 1], tile_oh[:, :, 2], bc(tcon[:, :], 2, [P, NT, ST]), ALU.mult))
                for t in range(NT - PO):
                    v.tensor_scalar(place_oh[:, t, :], placecon[:, :], slot_tp[:, 1, t:t + 1], None,
                                    ALU.is_equal).then_inc(s_place, 1)
                link(v.tensor_tensor(cmp[:, :, :], bc(small[:, 3], 1, [P, ST, E]), bc(jcon[:, :], 2, [P, ST, E]),
                                     ALU.is_le))
                link(v.tensor_reduce(texf[:, :], cmp[:, :, :], AX, ALU.add))
                link(v.tensor_scalar(tex[:, :], texf[:, :], float(E - 1), None, ALU.min))
                dve.wait_ge(s_ez, f + 1)
                link(v.tensor_scalar(eal[:, :], eal[:, :], 1.0, None, ALU.add))
                link(v.reciprocal(eal[:, :], eal[:, :]))
                link(v.tensor_scalar(half_alpha[:, :], eal[:, :], 0.5, None, ALU.mult))
                dve.wait_ge(s_inv, f + 1)
                link(v.tensor_copy(inv_sb[:, 0:2, :].rearrange("p k j -> p (k j)"), inv_ps))
                link(v.scalar_tensor_tensor(out=inv_sb[:, 2], in0=inv_sb[:, 1], scalar=float(P), in1=inv_sb[:, 0],
                                            op0=ALU.mult, op1=ALU.add))
                link(v.tensor_scalar(inv_sb[:, 3], inv_sb[:, 2], 0.0, None, ALU.is_equal))
                link(v.tensor_tensor(inv_sb[:, 4], inv_sb[:, 3], sparecon[:, :], ALU.mult))
                link(v.scalar_tensor_tensor(out=sidx[:, :], in0=inv_sb[:, 2], scalar=-1.0, in1=inv_sb[:, 4],
                                            op0=ALU.add, op1=ALU.add))
                v.tensor_scalar(gidx[:, :], inv_sb[:, 2], -1.0, 0.0, ALU.add, ALU.max).then_inc(s_idx, 1)
                if f == 0:
                    dve.wait_ge(s_w, 32)

                def fetch(j, s):
                    e = dve.value_load(tex[0:1, at(j, 1)], min_val=0, max_val=E - 1)
                    wait(dve, s_y, lin(j, 1, ST * f + 1 - WR))
                    wait(dve, s_ys, lin(j, 1, ST * f + 1 - WR))
                    v.tensor_copy(wcur[:, s, :], wall[:, bass.ds(e, 1), :].rearrange("p o w -> p (o w)")
                                  ).then_inc(s_wc, 1)

                def relu(j, s):
                    wait(dve, s_h, lin(j, 1, ST * f + 1))
                    wait(dve, s_y, lin(j, 1, ST * f + 1 - WR))
                    for c in (2, 3):
                        v.tensor_scalar(hT[:, s, c], hd_ps[j % 2][:, P * (c - 2):P * (c - 2) + P],
                                        wcur[:, s, O_B1 + c:O_B1 + c + 1], 0.0,
                                        ALU.add, ALU.max).then_inc(s_rd, 1)

                def result(j):
                    dve.wait_ge(s_y, ST * f + j + 1)
                    r = j % YR
                    wait(dve, s_yst[r], 16 * (uses(r, YR) * f + j // YR))
                    v.tensor_tensor(ys[:, r, :], y_ps[j % 2], wcur[:, j % WR, O_B2:PK], ALU.add).then_inc(s_ys, 1)

                fetch(0, 0)
                fetch(1, 1)
                for j in range(ST):
                    relu(j, j % WR)
                    if j + 2 < ST:
                        fetch(j + 2, (j + 2) % WR)
                    if j >= 1:
                        result(j - 1)
                    if j < NT:
                        v.tensor_scalar(X[:, j, :], X[:, j, :], xa[:, j:j + 1], xb[:, j:j + 1],
                                        ALU.mult, ALU.subtract).then_inc(s_aff, 1)
                result(ST - 1)
                dve.wait_ge(s_aff, NT * (f + 1))

            def combine(f, g):
                dve.wait_ge(s_g[g], 16 * (f + 1))
                for t in range(4 * g, 4 * g + 4):
                    v.scalar_tensor_tensor(out=X[:, t, :], in0=back[:, t, :], scalar=half_alpha[:, t:t + 1],
                                           in1=X[:, t, :], op0=ALU.mult, op1=ALU.add).then_inc(s_x1, 1)

            KN = 10
            own2 = s_own2

            def early(a, q, n):
                if n == 3:
                    for k in range(CT):
                        last = v.bn_stats(cst[:, k, :], X[:, at(a, CT, k, 1), :].rearrange("p o d -> p (o d)"))
                    step(last, a, 1)
                if n == 4:
                    for k, part in enumerate(moments(cst, cmom)):
                        step(part, a, 2 + k)
                if n == 5:
                    wait(dve, s_res, lin(a, 1, 0))
                    step(v.tensor_scalar(csm[:, 0], cmom[:, 3], EPS, None, ALU.add), a, 5)
                    step(v.reciprocal(csm[:, 6], csm[:, 0]), a, 6)
                if n == 6:
                    step(v.tensor_tensor(csm[:, 7], cmom[:, 3], csm[:, 6], ALU.mult), a, 7)
                    v.tensor_scalar(csm[:, 1], csm[:, 7], EPS, None, ALU.add).then_inc(s_cln, 1)
                if n == 9:
                    wait(dve, s_cr, lin(a, 1, 1))
                    step(v.tensor_tensor(csm[:, 7], csm[:, 4], csm[:, 5], ALU.mult), a, 8)
                    step(v.scalar_tensor_tensor(out=csm[:, 8], in0=csm[:, 4], scalar=-1.0, in1=cmom[:, 0],
                                                op0=ALU.mult, op1=ALU.mult), a, 9)
                    step(v.tensor_scalar(csm[:, 9], csm[:, 4], 1.0, None, ALU.add), a, 10)
                    v.scalar_tensor_tensor(out=csm[:, 10], in0=csm[:, 7], scalar=-1.0, in1=cmom[:, 0],
                                           op0=ALU.mult, op1=ALU.mult).then_inc(s_nb, 1)

            def late(b, q, n):
                if n in (7, 8, 9):
                    prep_split(b, q, n - 7)
                if n in (11, 12, 13):
                    prep_dt(b, q, n - 11)
                if n == 13:
                    dtx(b, q, 0)
                if n == 14:
                    dtx(b, q, 1)

            def step(ins, p, k):
                ins.then_inc(own2, 1)
                wait(dve, own2, lin(p, KN, k))

            def prep_split(p, q, k):
                mid = slice(96, 128)
                if k == 0:
                    wait(dve, s_hi, lin(p, 1, 1))
                    wait(dve, s_dtc, lin(p, 1, 1))
                    step3(v.tensor_tensor(bcr[mid, :], w_ps[0][mid, :], bcs[mid, q], ALU.subtract), p, 1)
                elif k == 1:
                    step3(v.tensor_copy(bcs[mid, q], bcr[mid, :]), p, 2)
                else:
                    v.tensor_tensor(bcs[0:32, q], bcr[mid, :], bcs[mid, q], ALU.subtract).then_inc(s_split, 1)

            def step3(ins, p, k):
                ins.then_inc(s_own3, 1)
                wait(dve, s_own3, lin(p, 2, k))

            def prep_dt(p, q, k):
                if k == 0:
                    for h in range(H2):
                        wait(dve, s_abs, lin(p, 2, h + 1))
                        v.tensor_scalar(dt[:, q, h], w_ps[h][:, :], wd2_b[:, h:h + 1], 0.0,
                                        ALU.add, ALU.max).then_inc(s_rz, 1)
                else:
                    h = k - 1
                    wait(dve, s_sp, lin(p, 2, h + 1))
                    wait(dve, s_rz, lin(p, 2, h + 1))
                    v.tensor_tensor(dt[:, q, h], dt[:, q, h], sp_t[:, h], ALU.add).then_inc(s_dt, 1)

            def dtx(p, q, h):
                wait(dve, s_dt, lin(p, 2, h + 1))
                wait(dve, s_xc, lin(p, 2, h + 1))
                v.tensor_tensor(u[:, q, h], dt[:, q, h], xc[:, q, h], ALU.mult).then_inc(s_u, 1)

            def dtxb(g, q, n):
                if n == 0:
                    wait(dve, s_u, lin(g, 2, 2))
                wait(dve, s_b, lin(g, NS, n + 1))
                wait(dve, s_scan, lin(g, 2 * NS, 2 * (n - 2) + 2))
                v.tensor_tensor(bu[:, n % 2], u[:, q], bc(b_ps[n % 2][:, :], 1, [P, H2, C]),
                                ALU.mult).then_inc(s_bu, 1)

            def save_carry(g, n):
                wait(dve, s_scan, lin(g, 2 * NS, 2 * n + 2))
                v.tensor_copy(carry[:, n, :], hb[:, n % 4, :, C - 1]).then_inc(s_car, 1)

            def scan(g, q, n):
                wait(dve, s_dA, lin(g, 2 * NS, 2 * n + 2))
                wait(dve, s_bu, lin(g, NS, n + 1))
                wait(dve, s_hc, lin(g, NS, n - 3))
                if q == 1:
                    if n == 0:
                        wait(dve, s_car, lin(g, NS // 2, NS // 2))
                for h in range(H2):
                    v.tensor_tensor_scan(out=hb[:, n % 4, h], data0=dA[:, n % 4, h], data1=bu[:, n % 2, h],
                                         initial=0.0 if q == 0 else carry[:, n, h:h + 1],
                                         op0=ALU.mult, op1=ALU.add).then_inc(s_scan, 1)

            def post_read(o, q):
                wait(dve, s_gate, lin(o, 1, 0))
                wait(dve, s_o, lin(o, 1, 0))
                wait(dve, s_acc, lin(o, 2 * NS, 2 * NS))
                for h in range(H2):
                    v.scalar_tensor_tensor(out=yg[:, h], in0=xc[:, q, h], scalar=w_D[:, h:h + 1],
                                           in1=acc_ps[h][:, :], op0=ALU.mult, op1=ALU.add).then_inc(s_yg, 1)

            def post_add(o):
                wait(dve, s_o, lin(o, 1, 1))
                wait(dve, s_res, lin(o, 1, 1))
                xk = X[:, at(o, CT), :]
                v.tensor_tensor(xk, xk, w_ps[1][:, :].rearrange("p (t d) -> p t d", d=D), ALU.add).then_inc(s_x2, 1)

            def post_stats(o):
                wait(dve, s_x2, lin(o, 1, 1))
                for k in range(CT):
                    ins = v.bn_stats(stat[:, at(o, CT, k, 1), :].rearrange("p o d -> p (o d)"),
                                     X[:, at(o, CT, k, 1), :].rearrange("p o d -> p (o d)"))
                ins.then_inc(s_stat, 1)

            def window(g, q, a, b, o):
                for n in range(NS):
                    if q == 0 and n >= 1:
                        save_carry(g, n - 1)
                    if n == 2 and o is not None:
                        post_read(o, 1 - q)
                    scan(g, q, n)
                    if n + 1 < NS:
                        dtxb(g, q, n + 1)
                    elif b is not None:
                        dtxb(b, 1 - q, 0)
                    if b is not None:
                        late(b, 1 - q, n)
                    if a is not None:
                        early(a, q, n)
                    if n == 10 and o is not None:
                        post_add(o)
                    if n == 14 and o is not None:
                        post_stats(o)
                if q == 0:
                    save_carry(g, NS - 1)

            ffn(0)
            combine(0, 0)
            dve.wait_ge(s_x1, 4)
            for n in range(NS):
                if n == 7:
                    combine(0, 1)
                early(0, 0, n)
            dve.wait_ge(s_x1, 8)
            for n in range(NS):
                late(0, 0, n)
                early(1, 1, n)
                if n < GR - 2:
                    combine(0, 2 + n)
            dve.wait_ge(s_x1, NT)
            dtxb(0, 0, 0)
            window(0, 0, 2, 1, None)
            with dve.Fori(0, LOOPS) as i:
                window((i, 2, 1), 1, (i, 2, 3), (i, 2, 2), (i, 2, 0))
                window((i, 2, 2), 0, (i, 2, 4), (i, 2, 3), (i, 2, 1))
            for g in range(2 * LOOPS + 1, NCH):
                window(g, g % 2, g + 2 if g + 2 < NCH else None, g + 1 if g + 1 < NCH else None, g - 1)
            post_read(NCH - 1, 1)
            post_add(NCH - 1)
            post_stats(NCH - 1)
            ffn(1)
            for g in range(GR):
                combine(1, g)


def kernel(**inputs):
    import numpy as np
    import concourse.bacc as bacc
    from concourse.bass_utils import run_bass_kernel_spmd as run

    i = {k: np.asarray(x) for k, x in inputs.items()}
    m = {k[len("L0_attn_"):]: x for k, x in i.items() if k.startswith("L0_attn_")}
    f = {k[len("L0_ffn_"):]: x for k, x in i.items() if k.startswith("L0_ffn_")}

    def halves(w):
        return w.reshape(2, 128, -1).transpose(1, 0, 2)

    arrays = {
        "x": m["resid"].reshape(4096, 128),
        "centT": f["centroids"].T,
        "experts": np.concatenate([
            f["W1"].transpose(2, 0, 1),
            f["W2"].reshape(8, 128, 4, 128).transpose(3, 0, 2, 1).reshape(128, 8, 512),
            f["b1"].reshape(8, 4, 128).transpose(2, 0, 1),
            f["gamma"].T[:, :, None], f["beta"].T[:, :, None]], axis=2),
        "b2": f["b2"],
        "par": np.concatenate([
            halves(m["A_log"]).reshape(128, 32),
            m["conv_b"].reshape(2, 128).T, m["wd2_b"].reshape(2, 128).T, m["W_D"].reshape(2, 128).T,
            m["norm_w"][:, None]], axis=1),
        "in_wT": m["in_w"].T,
        "skip_wT": m["skip_w"].T,
        "conv_wT": m["conv_w"].T,
        "wd2T": m["wd2"].T,
        "wrbcT": halves(np.concatenate([m["wd1"], m["wb"], m["wc"], m["wb"], m["wc"]], axis=0).T),
        "out_wT": halves(m["out_w"].T),
    }
    arrays = {k: np.ascontiguousarray(x) for k, x in arrays.items()}
    nc = bacc.Bacc("TRN2", target_bir_lowering=False, num_devices=1)
    aps = {k: nc.dram_tensor("in_" + k, x.shape, mybir.dt.float32, kind="ExternalInput").ap() for k, x in arrays.items()}
    out = nc.dram_tensor("out_y", (4096, 128), mybir.dt.float32, kind="ExternalOutput").ap()
    build(nc, aps, out)
    r = run(nc, [{"in_" + k: x for k, x in arrays.items()}], core_ids=[0])
    return r.results[0]["out_y"].reshape(4, 1024, 128)
```
